# Optimizing a Trainium2 kernel written in Bass

```python
import numpy as np
import jax
import jax.numpy as jnp

def _softmax(x, axis=-1):
    return jax.nn.softmax(x, axis=axis)

def _gelu(x):
    return jax.nn.gelu(x, approximate=True)

def _silu(x):
    return jax.nn.silu(x)

def _sigmoid(x):
    return jax.nn.sigmoid(x)

def _layernorm(x, axis=-1, eps=1e-05):
    m = jnp.mean(x, axis=axis, keepdims=True)
    v = jnp.var(x, axis=axis, keepdims=True)
    return (x - m) / jnp.sqrt(v + eps)

def _scatter_add(tgt, idx, src, axis=0):
    return tgt.at[idx].add(src)

def _segment_sum(src, seg, n):
    return jax.ops.segment_sum(src, seg, n)
kernel_name = 'mk_adj_resnorm_d2_adj_r2_382245'

def setup_inputs(seed: int=0):
    np.random.seed(seed)
    _w = jnp.asarray

    def _rec_inputs():
        import jax
        import jax.numpy as jnp
        _gk = jax.random.key(seed)
        x = -0.0004039 + 1 * jax.random.normal(jax.random.fold_in(_gk, 1), (128, 64, 384), jnp.float32)
        _a = jax.random.bernoulli(jax.random.fold_in(_gk, 2), 0.0625, (128, 64, 64))
        _a = jnp.logical_or(_a, jnp.swapaxes(_a, -1, -2))
        _a = jnp.logical_or(_a, jnp.eye(64, dtype=bool))
        _af = _a.astype(jnp.float32)
        adj = _af
        return (x, adj)
    x, adj = _rec_inputs()

    def _L0_gnn_setup():
        import jax, jax.numpy as jnp
        import numpy as np
        B, S, H, L = (32, 256, 384, 2)

        def _layer_norm(z, a, b, eps=0.001):
            mu = jnp.mean(z, axis=-1, keepdims=True)
            sigma = jnp.std(z, axis=-1, keepdims=True, ddof=1)
            return (z - mu) / (sigma + eps) * a + b
        key = jax.random.key(seed)
        ks = jax.random.split(key, 6)
        hidden_state = jax.random.normal(ks[0], (B, S, H), dtype=jnp.float32)
        adjacency_matrix = (jax.random.uniform(ks[1], (B, S, S)) < 0.2).astype(jnp.float32)
        W_left = 0.05 * jax.random.normal(ks[2], (L, H, H), dtype=jnp.float32)
        W_right = 0.05 * jax.random.normal(ks[3], (L, H, H), dtype=jnp.float32)
        W_lin = 0.05 * jax.random.normal(ks[4], (L, H, H), dtype=jnp.float32)
        b_lin = jnp.zeros((L, H), dtype=jnp.float32)
        ln_a = jnp.ones((L, H), dtype=jnp.float32)
        ln_b = jnp.zeros((L, H), dtype=jnp.float32)
        return {'hidden_state': hidden_state, 'adjacency_matrix': adjacency_matrix, 'W_left': W_left, 'W_right': W_right, 'W_lin': W_lin, 'b_lin': b_lin, 'ln_a': ln_a, 'ln_b': ln_b}
    _L0_gnn_all = _L0_gnn_setup()
    _L0_gnn_in = {k: v for k, v in _L0_gnn_all.items() if k in ('W_left', 'W_right', 'W_lin', 'b_lin', 'ln_a', 'ln_b')}
    del _L0_gnn_all

    def _L1_gnn_setup():
        import jax, jax.numpy as jnp
        import numpy as np
        LN_EPS = 1e-12

        def _digcn_forward(hidden_state, adjacency_matrix, Wl, bl, Ws, bs, Wr, br, ln_w, ln_b):
            B, S, D = hidden_state.shape
            temper = jnp.asarray(D, jnp.float32) ** 0.5
            i = jnp.arange(S)
            upper = (i[None, :] > i[:, None]).astype(hidden_state.dtype)
            lower = (i[None, :] < i[:, None]).astype(hidden_state.dtype)

            def layer(h, params):
                wl, b_l, ws, b_s, wr, b_r, g, beta = params
                u = jnp.einsum('bid,bjd->bij', h, h) / temper
                a = jax.nn.softmax(u, axis=-1)
                delta = a * adjacency_matrix
                attn = delta / (jnp.sum(delta, axis=-1, keepdims=True) + 1e-10)
                hl = h @ wl.T + b_l
                hs = h @ ws.T + b_s
                hr = h @ wr.T + b_r
                diag_a = jnp.diagonal(attn, axis1=1, axis2=2)
                ctx = jnp.einsum('bij,bjd->bid', attn * upper, hl) + diag_a[..., None] * hs + jnp.einsum('bij,bjd->bid', attn * lower, hr)
                mean = ctx.mean(-1, keepdims=True)
                var = ctx.var(-1, keepdims=True)
                o = (ctx - mean) / jnp.sqrt(var + LN_EPS) * g + beta
                return (jax.nn.relu(o), None)
            out, _ = jax.lax.scan(layer, hidden_state, (Wl, bl, Ws, bs, Wr, br, ln_w, ln_b))
            return out
        key = jax.random.key(seed)
        ks = jax.random.split(key, 6)
        B, S, D, L = (8, 512, 384, 2)
        scale = (1.0 / D) ** 0.5
        hidden_state = jax.random.normal(ks[0], (B, S, D), jnp.float32)
        adjacency_matrix = (jax.random.uniform(ks[1], (B, S, S)) < 0.05).astype(jnp.float32)
        Wl = jax.random.normal(ks[2], (L, D, D), jnp.float32) * scale
        Ws = jax.random.normal(ks[3], (L, D, D), jnp.float32) * scale
        Wr = jax.random.normal(ks[4], (L, D, D), jnp.float32) * scale
        bl = jnp.zeros((L, D), jnp.float32)
        bs = jnp.zeros((L, D), jnp.float32)
        br = jnp.zeros((L, D), jnp.float32)
        ln_w = jnp.ones((L, D), jnp.float32)
        ln_b = jnp.zeros((L, D), jnp.float32)
        return dict(hidden_state=hidden_state, adjacency_matrix=adjacency_matrix, Wl=Wl, bl=bl, Ws=Ws, bs=bs, Wr=Wr, br=br, ln_w=ln_w, ln_b=ln_b)
    _L1_gnn_all = _L1_gnn_setup()
    _L1_gnn_in = {k: v for k, v in _L1_gnn_all.items() if k in ('Wl', 'bl', 'Ws', 'bs', 'Wr', 'br', 'ln_w', 'ln_b')}
    del _L1_gnn_all
    return {'x': x, 'adj': adj, 'L0_gnn_W_left': _L0_gnn_in['W_left'], 'L0_gnn_W_right': _L0_gnn_in['W_right'], 'L0_gnn_W_lin': _L0_gnn_in['W_lin'], 'L0_gnn_b_lin': _L0_gnn_in['b_lin'], 'L0_gnn_ln_a': _L0_gnn_in['ln_a'], 'L0_gnn_ln_b': _L0_gnn_in['ln_b'], 'L1_gnn_Wl': _L1_gnn_in['Wl'], 'L1_gnn_bl': _L1_gnn_in['bl'], 'L1_gnn_Ws': _L1_gnn_in['Ws'], 'L1_gnn_bs': _L1_gnn_in['bs'], 'L1_gnn_Wr': _L1_gnn_in['Wr'], 'L1_gnn_br': _L1_gnn_in['br'], 'L1_gnn_ln_w': _L1_gnn_in['ln_w'], 'L1_gnn_ln_b': _L1_gnn_in['ln_b']}

def reference(x, adj, L0_gnn_W_left, L0_gnn_W_right, L0_gnn_W_lin, L0_gnn_b_lin, L0_gnn_ln_a, L0_gnn_ln_b, L1_gnn_Wl, L1_gnn_bl, L1_gnn_Ws, L1_gnn_bs, L1_gnn_Wr, L1_gnn_br, L1_gnn_ln_w, L1_gnn_ln_b):
    import jax
    import jax.numpy as jnp

    def _L0_gnn_ref(hidden_state, adjacency_matrix, W_left, W_right, W_lin, b_lin, ln_a, ln_b):
        import jax, jax.numpy as jnp
        import numpy as np
        B, S, H, L = (32, 256, 384, 2)

        def _layer_norm(z, a, b, eps=0.001):
            mu = jnp.mean(z, axis=-1, keepdims=True)
            sigma = jnp.std(z, axis=-1, keepdims=True, ddof=1)
            return (z - mu) / (sigma + eps) * a + b
        temper = float(np.sqrt(H))
        adj = adjacency_matrix
        adj_tri = jnp.triu(adj, k=1)
        diag_mask = jnp.triu(adj, k=0) - adj_tri
        h = hidden_state
        for l in range(L):
            m_left = jnp.einsum('bsh,oh->bso', h, W_left[l])
            m_right = jnp.einsum('bsh,oh->bso', h, W_right[l])
            u_left = jnp.einsum('bih,bjh->bij', h, m_left) / temper
            u_right = jnp.einsum('bih,bjh->bij', h, m_right) / temper
            u = u_left * adj_tri + u_left * diag_mask + u_right * jnp.swapaxes(adj_tri, 1, 2)
            delta_exp_u = jnp.exp(u) * adj
            attention = delta_exp_u / (jnp.sum(delta_exp_u, axis=2, keepdims=True) + 1e-10)
            h_lin = jnp.einsum('bsh,oh->bso', h, W_lin[l]) + b_lin[l]
            ctx = jnp.matmul(attention, h_lin)
            h = jax.nn.relu(_layer_norm(ctx, ln_a[l], ln_b[l]))
        return h

    def _L1_gnn_ref(hidden_state, adjacency_matrix, Wl, bl, Ws, bs, Wr, br, ln_w, ln_b):
        import jax, jax.numpy as jnp
        import numpy as np
        LN_EPS = 1e-12

        def _digcn_forward(hidden_state, adjacency_matrix, Wl, bl, Ws, bs, Wr, br, ln_w, ln_b):
            B, S, D = hidden_state.shape
            temper = jnp.asarray(D, jnp.float32) ** 0.5
            i = jnp.arange(S)
            upper = (i[None, :] > i[:, None]).astype(hidden_state.dtype)
            lower = (i[None, :] < i[:, None]).astype(hidden_state.dtype)

            def layer(h, params):
                wl, b_l, ws, b_s, wr, b_r, g, beta = params
                u = jnp.einsum('bid,bjd->bij', h, h) / temper
                a = jax.nn.softmax(u, axis=-1)
                delta = a * adjacency_matrix
                attn = delta / (jnp.sum(delta, axis=-1, keepdims=True) + 1e-10)
                hl = h @ wl.T + b_l
                hs = h @ ws.T + b_s
                hr = h @ wr.T + b_r
                diag_a = jnp.diagonal(attn, axis1=1, axis2=2)
                ctx = jnp.einsum('bij,bjd->bid', attn * upper, hl) + diag_a[..., None] * hs + jnp.einsum('bij,bjd->bid', attn * lower, hr)
                mean = ctx.mean(-1, keepdims=True)
                var = ctx.var(-1, keepdims=True)
                o = (ctx - mean) / jnp.sqrt(var + LN_EPS) * g + beta
                return (jax.nn.relu(o), None)
            out, _ = jax.lax.scan(layer, hidden_state, (Wl, bl, Ws, bs, Wr, br, ln_w, ln_b))
            return out
        return _digcn_forward(hidden_state, adjacency_matrix, Wl, bl, Ws, bs, Wr, br, ln_w, ln_b)
    x = _layernorm(x + _L0_gnn_ref(x, adj, L0_gnn_W_left, L0_gnn_W_right, L0_gnn_W_lin, L0_gnn_b_lin, L0_gnn_ln_a, L0_gnn_ln_b), axis=-1)
    x = _layernorm(x + _L1_gnn_ref(x, adj, L1_gnn_Wl, L1_gnn_bl, L1_gnn_Ws, L1_gnn_bs, L1_gnn_Wr, L1_gnn_br, L1_gnn_ln_w, L1_gnn_ln_b), axis=-1)
    return x

_drawn_inputs = setup_inputs


def setup_inputs(seed=0):
    import zlib

    import numpy as np

    out = dict(_drawn_inputs(seed))
    spreads = {'L0_gnn_b_lin': (0.0, 0.1),
     'L0_gnn_ln_a': (1.0, 0.2),
     'L0_gnn_ln_b': (0.0, 0.1),
     'L1_gnn_bl': (0.0, 0.8),
     'L1_gnn_bs': (0.0, 0.1),
     'L1_gnn_br': (0.0, 0.8),
     'L1_gnn_ln_w': (1.0, 0.2),
     'L1_gnn_ln_b': (0.0, 0.1)}
    factors = {'L1_gnn_Wl': 7.134, 'L1_gnn_Wr': 8.0}
    for name, (base, spread) in spreads.items():
        noise = np.random.default_rng([zlib.crc32(name.encode()), seed]).standard_normal(out[name].shape)
        drawn = base * np.exp(spread * noise) if base else spread * noise
        out[name] = jnp.asarray(drawn.astype(out[name].dtype))
    for name, factor in factors.items():
        out[name] = (out[name] * factor).astype(out[name].dtype)
    return out
```

```python
import numpy as np
import concourse.bass as bass
from concourse import mybir
from contextlib import ExitStack

F32 = mybir.dt.float32
F32R = mybir.dt.float32r
ALU = mybir.AluOpType
ACT = mybir.ActivationFunctionType
AX = mybir.AxisListType

GRAPHS, NODES, D = 128, 64, 384
LAYERS = 2
P = 128
KC = D // P
GT = 4
GROUPS = GRAPHS * NODES // (GT * P)
PAIR = 2
STEPS = GROUPS // PAIR
INST = LAYERS * PAIR
RING = 6
CREDIT = RING
HLW = D + 2
TEMPER = 1.0 / float(np.sqrt(D))
CROSS = -float(2.0 ** 100)
TERMS = ((0, 0), (0, 1), (1, 0))


def ring_plan(order):
    n, need = len(order), []
    last = {p % RING: p for p in range(n)}
    for p in range(n):
        prev = p - RING if p >= RING else last[p] - n
        need.append(prev + 1 + CREDIT)
    return {name: p for p, name in enumerate(order)}, need


def as_f32(ap):
    return ap.bitcast(F32)


def flat(ap):
    return ap.rearrange("p t i -> p (t i)")


def identity(pool, ident, zeroed, made):
    pool.memset(ident[:, :], 0.0).then_inc(zeroed, 1)
    pool.wait_ge(zeroed, 1)
    pool.affine_select(out=ident[:, :], in_=ident[:, :], compare_op=ALU.not_equal, fill=1.0, base=0,
                       pattern=[[-1, P]], channel_multiplier=1).then_inc(made, 1)


def network0(nc, x, adj, w_left, w_right, w_lin, b_lin, ln_a, ln_b, out):
    order = []
    for l in range(LAYERS):
        for g in range(PAIR):
            order += [("A", l, g, 0)] if l == 0 else []
            order += [("T", l, g, c) for c in range(KC)]
            order += [("N", l, g, i) for i in range(2 * KC)]
        for g in range(PAIR):
            order += [("H", l, g, t) for t in range(GT)]
            order += [("C", l, g, t) for t in range(GT)]
    job, need = ring_plan(order)
    JOBS = len(order)

    ctx = ExitStack()
    with ctx:
        def sb(name, shape, dt=F32):
            return ctx.enter_context(nc.sbuf_tensor("n0_" + name, shape, dt))

        def sem(name):
            return ctx.enter_context(nc.semaphore("n0_" + name))

        ident = sb("ident", [P, P])
        W = [[[sb(f"w{l}{m}{s}", [P, KC, D], F32R) for s in range(2)] for m in range(3)] for l in range(LAYERS)]
        bias, gain, beta = (sb(n, [P, LAYERS, D]) for n in ("bias", "gain", "beta"))
        X = [sb(f"x{g}", [P, GT, D]) for g in range(PAIR)]
        O = [sb(f"o{g}", [P, GT, D]) for g in range(PAIR)]
        stage = [X[1], O[1]]
        A = [sb(f"a{g}", [P, GT, P]) for g in range(PAIR)]
        AT = [sb(f"at{g}", [P, GT, P]) for g in range(PAIR)]
        SM = [sb(f"sm{g}", [P, GT, 2, P]) for g in range(PAIR)]
        HT = [[sb(f"ht{g}{s}", [P, KC, GT * P], F32R) for s in range(2)] for g in range(PAIR)]
        N = [sb(f"n{s}", [P, KC, 2, GT * P], F32R) for s in range(2)]
        HB = sb("hb", [P, 2, D])
        HL = [sb(f"hl{s}", [P, GT, HLW], F32R) for s in range(2)]
        UM = [sb(f"um{k}", [P, 2, 2, P]) for k in range(2)]
        E = sb("e", [P, GT, P])
        PR = [[sb(f"p{g}{s}", [P, GT, P], F32R) for s in range(2)] for g in range(PAIR)]
        half, mhalf = sb("half", [P, GT]), sb("mhalf", [P, GT])
        ST, MV = sb("st", [P, GT, 6]), sb("mv", [P, GT, 2])
        WS, SD, FC = sb("ws", [P, GT]), sb("sd", [P, GT]), sb("fc", [P, GT])
        ST2, MV2, VE, RS = sb("st2", [P, GT, 6]), sb("mv2", [P, GT, 2]), sb("ve", [P, GT]), sb("rs", [P, GT])
        scratch, scratch2 = sb("scratch", [P, 4]), sb("scratch2", [P, 4, GT])

        bank = [ctx.enter_context(nc.psum_tensor(f"n0_bank{i}", [P, 512], F32)) for i in range(RING)]
        ubank = [ctx.enter_context(nc.psum_tensor(f"n0_u{i}", [P, 512], F32)) for i in range(2)]

        bank_full = sem("bank_full")
        drained = sem("drained")
        x_in, a_in, x_free, a_free, stored = (
            [sem(f"{n}{g}") for g in range(PAIR)] for n in ("x_in", "a_in", "x_free", "a_free", "stored"))
        ht_hi, n_hi = sem("ht_hi"), sem("n_hi")
        u_full, u_masked, u_added = sem("u_full"), sem("u_masked"), sem("u_added")
        e_done, p_done, p_hi, p_lo = sem("e_done"), sem("p_done"), sem("p_hi"), sem("p_lo")
        hl_hi, hl_lo = sem("hl_hi"), sem("hl_lo")
        var_ready, sd_ready, o_ready, var2_ready, rs_ready, o_out = (
            sem(n) for n in ("var_ready", "sd_ready", "o_ready", "var2_ready", "rs_ready", "o_out"))
        v_done = sem("v_done")
        w_in = [sem("w_in0"), sem("w_in1")]
        c_in, w_hi, w_lo, w_t, zeroed, made = (sem(n) for n in ("c_in", "w_hi", "w_lo", "w_t", "zeroed", "made"))
        MADE = 4

        xg = x.rearrange("(g t p) d -> g p t d", p=P, t=GT)
        og = out.rearrange("(g t p) d -> g p t d", p=P, t=GT)
        ag = adj.rearrange("(g t q) j i -> g q j t i", q=2, t=GT)
        mats = [(w, l, m) for l in range(LAYERS) for m, w in enumerate((w_left[l], w_right[l], w_lin[l]))]
        TRANSPOSED = 2

        block = ctx.enter_context(nc.Block())

        @block.sync
        def _(sp):
            def weight(m):
                sp.dma_start(stage[m % 2][:, 0:KC, :], mats[m][0].rearrange("(k p) h -> p k h", p=P)).then_inc(w_in[m % 2], 16)

            def load(step, g, first=False):
                if not first:
                    sp.wait_ge(x_free[g], step)
                sp.dma_start(X[g][:, :, :], xg[step * PAIR + g]).then_inc(x_in[g], 16)
                if not first:
                    sp.wait_ge(a_free[g], step)
                for q in range(2):
                    sp.dma_start(A[g][q * NODES:(q + 1) * NODES, :, q * NODES:(q + 1) * NODES],
                                 ag[step * PAIR + g][q]).then_inc(a_in[g], 16)

            def store(step, g):
                sp.wait_ge(o_out, step * PAIR + g + 1)
                sp.dma_start(og[step * PAIR + g], O[g][:, :, :]).then_inc(stored[g], 16)

            weight(0)
            weight(1)
            for l in range(LAYERS):
                for dst, src in ((bias, b_lin), (gain, ln_a), (beta, ln_b)):
                    sp.dma_start(dst[:, l], src[l].partition_broadcast(P)).then_inc(c_in, 16)
            sp.wait_ge(made, MADE)
            load(0, 0, first=True)
            for m in range(2, len(mats)):
                sp.wait_ge(w_lo, m - 1)
                weight(m)
            sp.wait_ge(w_lo, len(mats))
            load(0, 1, first=True)
            with sp.Fori(0, STEPS - 1, 1) as it:
                for g in range(PAIR):
                    load(it + 1, g)
                    store(it, g)
            for g in range(PAIR):
                store(STEPS - 1, g)
            for g in range(PAIR):
                sp.wait_ge(stored[g], (STEPS + 1) * 16)

        @block.tensor
        def _(pe):
            pe.wait_ge(made, MADE)
            for m, (_, l, kind) in enumerate(mats):
                if kind == TRANSPOSED:
                    pe.wait_ge(w_in[m % 2], 16 * (m // 2 + 1))
                    pe.wait_ge(w_lo, m - 1)
                    for c in range(KC):
                        for k in range(KC):
                            last = pe.transpose(bank[c][:, k * P:(k + 1) * P], stage[m % 2][:, k, c * P:(c + 1) * P], ident[:, :])
                    last.then_inc(w_t, 1)
            pe.wait_ge(w_lo, len(mats))
            with pe.Fori(0, STEPS, 1) as it:
                def free(p):
                    pe.wait_ge(drained, it * JOBS + need[p])

                def result(name):
                    pe.wait_ge(drained, it * JOBS + (job[name] + 1 + CREDIT))

                for l in range(LAYERS):
                    for g in range(PAIR):
                        n = it * INST + (l * PAIR + g)
                        if l == 0:
                            p = job["A", l, g, 0]
                            pe.wait_ge(a_in[g], (it + 1) * 32)
                            free(p)
                            for t in range(GT):
                                last = pe.transpose(bank[p % RING][:, t * P:(t + 1) * P], A[g][:, t, :], ident[:, :])
                            last.then_inc(bank_full, 1)
                            pe.wait_ge(x_in[g], (it + 1) * 16)
                        else:
                            pe.wait_ge(o_ready, it * PAIR + g + 1)
                        src = X[g] if l == 0 else O[g]
                        for c in range(KC):
                            p = job["T", l, g, c]
                            free(p)
                            for t in range(GT):
                                last = pe.transpose(bank[p % RING][:, t * P:(t + 1) * P], src[:, t, c * P:(c + 1) * P], ident[:, :])
                            last.then_inc(bank_full, 1)
                        for i in range(2 * KC):
                            side, c = i // KC, i % KC
                            p = job["N", l, g, i]
                            free(p)
                            for k in range(KC):
                                if i == 0:
                                    result(("T", l, g, k))
                                for j, (a, b) in enumerate(TERMS):
                                    last = pe.matmul(bank[p % RING][:, :], lhsT=W[l][side][a][:, k, c * P:(c + 1) * P],
                                                     rhs=HT[g][b][:, k, :], start=(k == 0 and j == 0), stop=(k == KC - 1 and j == 2))
                            last.then_inc(bank_full, 1)
                        result(("N", l, g, 2 * KC - 1))
                        for k in range(2):
                            pe.wait_ge(u_masked, n * 2 + (k + 1))
                            for t in range(2):
                                cols = slice((2 * k + t) * P, (2 * k + t + 1) * P)
                                for c in range(KC):
                                    for j, (a, b) in enumerate(TERMS):
                                        last = pe.matmul(ubank[k][:, t * 2 * P:(t + 1) * 2 * P], lhsT=HT[g][a][:, c, cols],
                                                         rhs=N[b][:, c, :, cols], start=(c == 0 and j == 0), stop=(c == KC - 1 and j == 2))
                            last.then_inc(u_full, 1)
                    for g in range(PAIR):
                        n = it * INST + (l * PAIR + g)
                        for t in range(GT):
                            p = job["H", l, g, t]
                            free(p)
                            for c in range(KC):
                                for j, (a, b) in enumerate(TERMS):
                                    last = pe.matmul(bank[p % RING][:, 0:D], lhsT=HT[g][a][:, c, t * P:(t + 1) * P],
                                                     rhs=W[l][2][b][:, c, :], start=(c == 0 and j == 0), stop=(c == KC - 1 and j == 2))
                            last.then_inc(bank_full, 1)
                        for t in range(GT):
                            p = job["C", l, g, t]
                            free(p)
                            pe.wait_ge(p_lo, n * 2 + (t // 2 + 1 + 2))
                            pe.wait_ge(hl_lo, n * GT + (t + 1 + 2))
                            for j, (a, b) in enumerate(TERMS):
                                last = pe.matmul(bank[p % RING][:, 0:HLW], lhsT=PR[g][a][:, t, :], rhs=HL[b][:, t, :],
                                                 start=(j == 0), stop=(j == 2))
                            last.then_inc(bank_full, 1)

        @block.scalar
        def _(act):
            for m, (_, l, kind) in enumerate(mats):
                if kind == TRANSPOSED:
                    act.wait_ge(w_t, l + 1)
                    for c in range(KC):
                        last = act.activation(W[l][kind][0][:, c, :], bank[c][:, 0:D], ACT.Copy)
                else:
                    act.wait_ge(w_in[m % 2], 16 * (m // 2 + 1))
                    last = act.activation(W[l][kind][0][:, :, :], stage[m % 2][:, 0:KC, :], ACT.Copy)
                last.then_inc(w_hi, 1)

            with act.Fori(0, STEPS, 1) as it:
                def split_t(l, g):
                    for c in range(KC):
                        p = job["T", l, g, c]
                        act.wait_ge(bank_full, it * JOBS + (p + 1))
                        act.activation(HT[g][0][:, c, :], bank[p % RING][:, :], ACT.Relu if l else ACT.Copy).then_inc(ht_hi, 1)

                def split_n(l, g):
                    for i in range(2 * KC):
                        p = job["N", l, g, i]
                        act.wait_ge(bank_full, it * JOBS + (p + 1))
                        act.activation(N[0][:, i % KC, i // KC, :], bank[p % RING][:, :], ACT.Copy).then_inc(n_hi, 1)

                def exps(l, g):
                    n = it * INST + (l * PAIR + g)
                    for k in range(2):
                        act.wait_ge(u_added, n * 2 + (k + 1 + 2))
                        act.activation(E[:, 2 * k:2 * k + 2, :], E[:, 2 * k:2 * k + 2, :], ACT.Exp, scale=TEMPER).then_inc(e_done, 1)

                def split_p(l, g):
                    n = it * INST + (l * PAIR + g)
                    for k in range(2):
                        act.wait_ge(p_done, n * 2 + (k + 1 + 2))
                        act.activation(PR[g][0][:, 2 * k:2 * k + 2, :], E[:, 2 * k:2 * k + 2, :], ACT.Copy).then_inc(p_hi, 1)

                def split_h(l, g):
                    for t in range(GT):
                        act.wait_ge(drained, it * JOBS + (job["H", l, g, t] + 1 + CREDIT))
                        act.activation(HL[0][:, t, 0:D], HB[:, t % 2, :], ACT.Copy).then_inc(hl_hi, 1)

                for l in range(LAYERS):
                    split_t(l, 0)
                    split_n(l, 0)
                    split_t(l, 1)
                    exps(l, 0)
                    split_n(l, 1)
                    split_p(l, 0)
                    split_h(l, 0)
                    exps(l, 1)
                    split_p(l, 1)
                    split_h(l, 1)

        @block.gpsimd
        def _(pool):
            identity(pool, ident, zeroed, made)
            for g in range(PAIR):
                pool.memset(A[g][:, :, :], 0.0).then_inc(made, 1)
            pool.memset(half[:, :], 0.5).then_inc(p_done, 2)
            pool.memset(scratch2[:, :, :], 0.0).then_inc(u_added, 2)
            pool.memset(mhalf[:, :], -0.5).then_inc(made, 1)
            pool.wait_ge(made, MADE)
            pool.memset(as_f32(HL[1][:, :, D:HLW]), 0.0).then_inc(p_lo, 2)
            pool.memset(as_f32(HL[0][:, :, D:HLW]), 1.0).then_inc(hl_lo, 2)

            with pool.Fori(0, STEPS, 1) as it:
                def carry_wait(k):
                    pool.tensor_tensor(scratch2[:, k, :], half[:, :], half[:, :], ALU.mult)

                def masks(g):
                    pool.wait_ge(a_in[g], (it + 1) * 32)
                    pool.wait_ge(u_masked, it * (INST * 2) + 2)
                    carry_wait(2 * g)
                    pool.affine_select(out=SM[g][:, :, 1, :], in_=A[g][:, :, :], compare_op=ALU.is_gt, fill=0.0, base=0,
                                       pattern=[[0, GT], [1, P]], channel_multiplier=-1)
                    pool.wait_ge(drained, it * JOBS + (job["A", 0, g, 0] + 1 + CREDIT))
                    carry_wait(2 * g + 1)
                    pool.affine_select(out=SM[g][:, :, 0, :], in_=AT[g][:, :, :], compare_op=ALU.is_ge, fill=0.0, base=0,
                                       pattern=[[0, GT], [-1, P]], channel_multiplier=1).then_inc(a_free[g], 1)

                def add_scores(l, g):
                    n = it * INST + (l * PAIR + g)
                    pool.wait_ge(p_lo, n * 2 + 2)
                    for k in range(2):
                        pool.wait_ge(u_masked, n * 2 + (k + 1 + 2))
                        pool.tensor_tensor(E[:, 2 * k:2 * k + 2, :], UM[k][:, :, 0, :], UM[k][:, :, 1, :], ALU.add).then_inc(u_added, 1)

                def mask_exp(l, g):
                    n = it * INST + (l * PAIR + g)
                    for k in range(2):
                        pool.wait_ge(e_done, n * 2 + (k + 1))
                        pool.tensor_tensor(E[:, 2 * k:2 * k + 2, :], E[:, 2 * k:2 * k + 2, :], AT[g][:, 2 * k:2 * k + 2, :],
                                           ALU.mult).then_inc(p_done, 1)

                def split_p(l, g):
                    n = it * INST + (l * PAIR + g)
                    for k in range(2):
                        pool.wait_ge(p_hi, n * 2 + (k + 1))
                        pool.tensor_tensor(PR[g][1][:, 2 * k:2 * k + 2, :], E[:, 2 * k:2 * k + 2, :],
                                           as_f32(PR[g][0][:, 2 * k:2 * k + 2, :]), ALU.subtract).then_inc(p_lo, 1)

                def split_h(l, g):
                    n = it * INST + (l * PAIR + g)
                    for t in range(GT):
                        pool.wait_ge(hl_hi, n * GT + (t + 1))
                        pool.tensor_tensor(HL[1][:, t, 0:D], HB[:, t % 2, :], as_f32(HL[0][:, t, 0:D]), ALU.subtract).then_inc(hl_lo, 1)

                def deviation(l, g):
                    pool.wait_ge(var_ready, it * INST + (l * PAIR + g + 1))
                    pool.tensor_tensor(SD[:, :], MV[:, :, 1], half[:, :], ALU.pow).then_inc(sd_ready, 1)

                def final_deviation(g):
                    pool.wait_ge(var2_ready, it * PAIR + (g + 1))
                    pool.tensor_tensor(RS[:, :], VE[:, :], mhalf[:, :], ALU.pow).then_inc(rs_ready, 1)

                for l in range(LAYERS):
                    if l == 0:
                        masks(0)
                        masks(1)
                    add_scores(l, 0)
                    mask_exp(l, 0)
                    split_p(l, 0)
                    split_h(l, 0)
                    add_scores(l, 1)
                    mask_exp(l, 1)
                    split_p(l, 1)
                    deviation(l, 0)
                    split_h(l, 1)
                    if l == LAYERS - 1:
                        final_deviation(0)
                    deviation(l, 1)
                    if l == LAYERS - 1:
                        final_deviation(1)

        V_STEPS = INST * (3 * GT - 1 + 2) + PAIR * (4 * GT - 1)

        @block.vector
        def _(dve):
            for m, (_, l, kind) in enumerate(mats):
                dve.wait_ge(w_hi, m + 1)
                if kind == TRANSPOSED:
                    for c in range(KC):
                        last = dve.tensor_tensor(W[l][kind][1][:, c, :], bank[c][:, 0:D], as_f32(W[l][kind][0][:, c, :]), ALU.subtract)
                else:
                    last = dve.tensor_tensor(W[l][kind][1][:, :, :], stage[m % 2][:, 0:KC, :], as_f32(W[l][kind][0][:, :, :]), ALU.subtract)
                last.then_inc(w_lo, 1)
            dve.wait_ge(c_in, 16 * 3 * LAYERS)
            dve.memset(scratch[:, 0:1], 0.0).then_inc(drained, CREDIT)
            dve.memset(scratch[:, 1:2], 0.0).then_inc(u_masked, 2)
            for g in range(PAIR):
                dve.memset(scratch[:, 2 + g:3 + g], 0.0).then_inc(stored[g], 16)

            with dve.Fori(0, STEPS, 1) as it:
                count = [0]

                def step(ins):
                    count[0] += 1
                    ins.then_inc(v_done, 1)
                    return count[0]

                def own(k):
                    dve.wait_ge(v_done, it * V_STEPS + k)

                def full(*name):
                    p = job[name]
                    dve.wait_ge(bank_full, it * JOBS + (p + 1))
                    return bank[p % RING]

                def masks(g):
                    dve.wait_ge(p_done, it * (INST * 2) + 2)
                    dve.tensor_copy(flat(AT[g][:, :, :]), full("A", 0, g, 0)[:, :]).then_inc(drained, 1)

                def split_t(l, g):
                    for c in range(KC):
                        ps = full("T", l, g, c)
                        dve.wait_ge(ht_hi, (it * INST + (l * PAIR + g)) * KC + (c + 1))
                        hi, lo = as_f32(HT[g][0][:, c, :]), HT[g][1][:, c, :]
                        if l == 0:
                            dve.tensor_tensor(lo, ps[:, :], hi, ALU.subtract).then_inc(drained, 1)
                        else:
                            dve.scalar_tensor_tensor(lo, ps[:, :], 0.0, hi, ALU.max, ALU.subtract).then_inc(drained, 1)

                def split_n(l, g):
                    for i in range(2 * KC):
                        ps = full("N", l, g, i)
                        dve.wait_ge(n_hi, (it * INST + (l * PAIR + g)) * (2 * KC) + (i + 1))
                        dve.tensor_tensor(N[1][:, i % KC, i // KC, :], ps[:, :], as_f32(N[0][:, i % KC, i // KC, :]),
                                          ALU.subtract).then_inc(drained, 1)

                def mask_scores(l, g):
                    n = it * INST + (l * PAIR + g)
                    dve.wait_ge(u_added, n * 2 + 2)
                    if l == 0:
                        dve.wait_ge(a_free[g], it + 1)
                    for k in range(2):
                        dve.wait_ge(u_full, n * 2 + (k + 1))
                        dve.tensor_tensor(UM[k][:, :, :, :].rearrange("p t s i -> p (t s i)"), ubank[k][:, :],
                                          SM[g][:, 2 * k:2 * k + 2, :, :].rearrange("p t s i -> p (t s i)"),
                                          ALU.mult).then_inc(u_masked, 1)

                def add_bias(l, g):
                    for t in range(GT):
                        ps = full("H", l, g, t)
                        dve.wait_ge(hl_lo, (it * INST + (l * PAIR + g)) * GT + (t + 1))
                        dve.tensor_tensor(HB[:, t % 2, :], ps[:, 0:D], bias[:, l, :], ALU.add).then_inc(drained, 1)

                def statistics(l, g):
                    if l == 0:
                        dve.wait_ge(stored[g], it * 16 + 16)
                    for t0 in range(0, GT, 2):
                        s, a = {}, {}
                        for t in (t0, t0 + 1):
                            s[t] = step(dve.bn_stats(ST[:, t, :], full("C", l, g, t)[:, 0:D]))
                        own(s[t0 + 1])
                        for t in (t0, t0 + 1):
                            w = step(dve.tensor_scalar(WS[:, t:t + 1], full("C", l, g, t)[:, D:D + 1], 1e-10, 1e-3, ALU.add, ALU.mult))
                        for t in (t0, t0 + 1):
                            ins = dve.bn_aggr(MV[:, t, :], ST[:, t, :])
                            if t == GT - 1:
                                ins.then_inc(var_ready, 1)
                            else:
                                a[t] = step(ins)
                        for t in (t0, t0 + 1):
                            if t == GT - 1:
                                dve.wait_ge(var_ready, it * INST + (l * PAIR + g + 1))
                            else:
                                own(a[t])
                            ps = full("C", l, g, t)
                            dve.scalar_tensor_tensor(O[g][:, t, :], ps[:, 0:D], MV[:, t, 0:1], gain[:, l, :],
                                                     ALU.subtract, ALU.mult).then_inc(drained, 1)

                def finish(l, g):
                    dve.wait_ge(sd_ready, it * INST + (l * PAIR + g + 1))
                    k = step(dve.scalar_tensor_tensor(FC[:, :], SD[:, :], float(np.sqrt(D / (D - 1.0))), WS[:, :], ALU.mult, ALU.add))
                    own(k)
                    k = step(dve.reciprocal(FC[:, :], FC[:, :]))
                    own(k)
                    dve.wait_ge(drained, it * JOBS + (job["C", l, g, GT - 1] + 1 + CREDIT))
                    s = {}
                    for t in range(GT):
                        ins = dve.scalar_tensor_tensor(O[g][:, t, :], O[g][:, t, :], FC[:, t:t + 1], beta[:, l, :], ALU.mult, ALU.add)
                        if l == LAYERS - 1:
                            s[t] = step(ins)
                    if l < LAYERS - 1:
                        ins.then_inc(o_ready, 1)
                        return
                    for t in range(GT):
                        own(s[t])
                        s[t] = step(dve.scalar_tensor_tensor(O[g][:, t, :], O[g][:, t, :], 0.0, X[g][:, t, :], ALU.max, ALU.add))
                    for t in range(GT):
                        own(s[t])
                        ins = dve.bn_stats(ST2[:, t, :], O[g][:, t, :])
                        if t == GT - 1:
                            ins.then_inc(x_free[g], 1)
                        else:
                            s[t] = step(ins)
                    dve.wait_ge(x_free[g], it + 1)
                    dve.tensor_scalar(scratch[:, 2 + g:3 + g], FC[:, 0:1], 0.0, None, ALU.mult)
                    for t in range(GT):
                        s[t] = step(dve.bn_aggr(MV2[:, t, :], ST2[:, t, :]))
                    own(s[GT - 1])
                    dve.tensor_scalar(VE[:, :], MV2[:, :, 1], 1e-5, None, ALU.add).then_inc(var2_ready, 1)

                def normalise(g):
                    dve.wait_ge(rs_ready, it * PAIR + (g + 1))
                    for t in range(GT):
                        ins = dve.tensor_scalar(O[g][:, t, :], O[g][:, t, :], MV2[:, t, 0:1], RS[:, t:t + 1], ALU.subtract, ALU.mult)
                    ins.then_inc(o_out, 1)

                for l in range(LAYERS):
                    last_layer = l == LAYERS - 1
                    for g in range(PAIR):
                        if l == 0:
                            masks(g)
                        split_t(l, g)
                        split_n(l, g)
                        mask_scores(l, g)
                    add_bias(l, 0)
                    statistics(l, 0)
                    add_bias(l, 1)
                    finish(l, 0)
                    statistics(l, 1)
                    if last_layer:
                        normalise(0)
                    finish(l, 1)
                    if last_layer:
                        normalise(1)
                assert count[0] == V_STEPS, (count[0], V_STEPS)


def network1(nc, x, adj, w_upper, b_upper, w_self, b_self, w_lower, b_lower, ln_w, ln_b, out):
    UPPER, LOWER, SELF = range(3)
    order = []
    for l in range(LAYERS):
        for g in range(PAIR):
            order += [("A", l, g, 0)] if l == 0 else []
            order += [("T", l, g, c) for c in range(KC)]
            if g == 1:
                order += [("C", l, 0, t) for t in range(GT)]
            order += [("R", l, g, (t, m)) for t in range(GT) for m in (UPPER, LOWER, SELF)]
        order += [("C", l, 1, t) for t in range(GT)]
    job, need = ring_plan(order)
    JOBS = len(order)
    SLOTS = 4

    ctx = ExitStack()
    with ctx:
        def sb(name, shape, dt=F32):
            return ctx.enter_context(nc.sbuf_tensor("n1_" + name, shape, dt))

        def sem(name):
            return ctx.enter_context(nc.semaphore("n1_" + name))

        ident, identr, ones = sb("ident", [P, P]), sb("identr", [P, P], F32R), sb("ones", [P, P], F32R)
        cross = sb("cross", [P, GT, P], F32R)
        W = [[[sb(f"w{l}{m}{s}", [P, KC, D], F32R) for s in range(2)] for m in range(3)] for l in range(LAYERS)]
        bias = sb("bias", [P, LAYERS, 3, D])
        gain, beta = (sb(n, [P, LAYERS, D]) for n in ("gain", "beta"))
        X = [sb(f"x{g}", [P, GT, D]) for g in range(PAIR)]
        O = [sb(f"o{g}", [P, GT, D]) for g in range(PAIR)]
        stage = [X[1], O[1]]
        A = [sb(f"a{g}", [P, GT, P]) for g in range(PAIR)]
        AT = sb("at", [P, GT, P])
        AM = [sb(f"am{g}", [P, 3, GT, P]) for g in range(PAIR)]
        HT = [[sb(f"ht{g}{s}", [P, KC, GT * P], F32R) for s in range(2)] for g in range(PAIR)]
        HB = sb("hb", [P, SLOTS, D])
        HL = [sb(f"hl{s}", [P, 2, GT, HLW], F32R) for s in range(2)]
        HS = sb("hs", [P, GT, D])
        MX, SH = sb("mx", [P, GT]), sb("sh", [P, GT, P], F32R)
        E = sb("e", [P, GT, P])
        EM = sb("em", [P, 2, GT, P])
        ES, DG = sb("es", [P, GT, P]), sb("dg", [P, GT])
        PR = [sb(f"p{s}", [P, 2, GT, P], F32R) for s in range(2)]
        ones2 = sb("ones2", [P, 2])
        mhalf = sb("mhalf", [P, GT])
        ST, MV = sb("st", [P, GT, 6]), sb("mv", [P, GT, 2])
        SS, DEN, D2, VV, FC = (sb(n, [P, GT]) for n in ("ss", "den", "d2", "vv", "fc"))
        ST2, MV2, VE, RS = sb("st2", [P, GT, 6]), sb("mv2", [P, GT, 2]), sb("ve", [P, GT]), sb("rs", [P, GT])
        scratch, scratch2 = sb("scratch", [P, 8]), sb("scratch2", [P, 4, GT])

        bank = [ctx.enter_context(nc.psum_tensor(f"n1_bank{i}", [P, 512], F32)) for i in range(RING)]
        ubank = [ctx.enter_context(nc.psum_tensor(f"n1_u{i}", [P, 512], F32)) for i in range(PAIR)]

        bank_full = sem("bank_full")
        drained = sem("drained")
        x_in, a_in, x_free, a_free, stored = (
            [sem(f"{n}{g}") for g in range(PAIR)] for n in ("x_in", "a_in", "x_free", "a_free", "stored"))
        ht_hi, u_full, u_shifted, z_full, z_read = (sem(n) for n in ("ht_hi", "u_full", "u_shifted", "z_full", "z_read"))
        shift_ready, e_done, em_done, es_done, dg_done, p_hi, p_lo = (
            sem(n) for n in ("shift_ready", "e_done", "em_done", "es_done", "dg_done", "p_hi", "p_lo"))
        hl_hi, hl_lo = sem("hl_hi"), sem("hl_lo")
        var_ready, sd_ready, o_ready, var2_ready, rs_ready, o_out = (
            sem(n) for n in ("var_ready", "sd_ready", "o_ready", "var2_ready", "rs_ready", "o_out"))
        v_done = sem("v_done")
        w_in = [sem("w_in0"), sem("w_in1")]
        c_in, w_hi, w_lo, w_t, zeroed, made = (sem(n) for n in ("c_in", "w_hi", "w_lo", "w_t", "zeroed", "made"))
        MADE = 4
        identr_made, cross_made = sem("identr_made"), sem("cross_made")

        xg = x.rearrange("(g t p) d -> g p t d", p=P, t=GT)
        og = out.rearrange("(g t p) d -> g p t d", p=P, t=GT)
        ag = adj.rearrange("(g t q) j i -> g q j t i", q=2, t=GT)
        mats = [(w, l, m) for l in range(LAYERS) for m, w in enumerate((w_upper[l], w_lower[l], w_self[l]))]

        block = ctx.enter_context(nc.Block())

        @block.sync
        def _(sp):
            def weight(m):
                sp.dma_start(stage[m % 2][:, 0:KC, :], mats[m][0].rearrange("(k p) h -> p k h", p=P)).then_inc(w_in[m % 2], 16)

            def load(step, g, first=False):
                if not first:
                    sp.wait_ge(x_free[g], step)
                sp.dma_start(X[g][:, :, :], xg[step * PAIR + g]).then_inc(x_in[g], 16)
                if not first:
                    sp.wait_ge(a_free[g], step)
                for q in range(2):
                    sp.dma_start(A[g][q * NODES:(q + 1) * NODES, :, q * NODES:(q + 1) * NODES],
                                 ag[step * PAIR + g][q]).then_inc(a_in[g], 16)

            def store(step, g):
                sp.wait_ge(o_out, step * PAIR + g + 1)
                sp.dma_start(og[step * PAIR + g], O[g][:, :, :]).then_inc(stored[g], 16)

            weight(0)
            weight(1)
            for l in range(LAYERS):
                for dst, src in ((bias[:, l, UPPER], b_upper), (bias[:, l, LOWER], b_lower), (bias[:, l, SELF], b_self),
                                 (gain[:, l], ln_w), (beta[:, l], ln_b)):
                    sp.dma_start(dst, src[l].partition_broadcast(P)).then_inc(c_in, 16)
            sp.wait_ge(made, MADE)
            load(0, 0, first=True)
            for m in range(2, len(mats)):
                sp.wait_ge(w_lo, m - 1)
                weight(m)
            sp.wait_ge(w_lo, len(mats))
            load(0, 1, first=True)
            with sp.Fori(0, STEPS - 1, 1) as it:
                for g in range(PAIR):
                    load(it + 1, g)
                    store(it, g)
            for g in range(PAIR):
                store(STEPS - 1, g)
            for g in range(PAIR):
                sp.wait_ge(stored[g], (STEPS + 1) * 16)

        @block.tensor
        def _(pe):
            pe.wait_ge(made, MADE)
            for m, (_, l, kind) in enumerate(mats):
                pe.wait_ge(w_in[m % 2], 16 * (m // 2 + 1))
                if m >= 2:
                    pe.wait_ge(w_lo, m - 1)
                for c in range(KC):
                    for k in range(KC):
                        last = pe.transpose(bank[m % 2 * KC + c][:, k * P:(k + 1) * P], stage[m % 2][:, k, c * P:(c + 1) * P], ident[:, :])
                last.then_inc(w_t, 1)
            pe.wait_ge(w_lo, len(mats))
            pe.wait_ge(identr_made, 1)
            pe.wait_ge(cross_made, 2)
            with pe.Fori(0, STEPS, 1) as it:
                def free(p):
                    pe.wait_ge(drained, it * JOBS + need[p])

                def head(l, g):
                    if l == 0:
                        p = job["A", l, g, 0]
                        pe.wait_ge(a_in[g], (it + 1) * 32)
                        free(p)
                        for t in range(GT):
                            last = pe.transpose(bank[p % RING][:, t * P:(t + 1) * P], A[g][:, t, :], ident[:, :])
                        last.then_inc(bank_full, 1)
                        pe.wait_ge(x_in[g], (it + 1) * 16)
                    else:
                        pe.wait_ge(o_ready, it * PAIR + g + 1)
                    src = X[g] if l == 0 else O[g]
                    for c in range(KC):
                        p = job["T", l, g, c]
                        free(p)
                        for t in range(GT):
                            last = pe.transpose(bank[p % RING][:, t * P:(t + 1) * P], src[:, t, c * P:(c + 1) * P], ident[:, :])
                        last.then_inc(bank_full, 1)

                def scores(l, g):
                    n = it * INST + (l * PAIR + g)
                    pe.wait_ge(z_read, n + 1)
                    pe.matmul(ubank[g][:, :], lhsT=identr[:, :], rhs=flat(cross[:, :, :]), start=True, stop=True)
                    for c in range(KC):
                        pe.wait_ge(drained, it * JOBS + (job["T", l, g, c] + 1 + CREDIT))
                        for t in range(GT):
                            cols = slice(t * P, (t + 1) * P)
                            for j, (a, b) in enumerate(TERMS):
                                last = pe.matmul(ubank[g][:, cols], lhsT=HT[g][a][:, c, cols], rhs=HT[g][b][:, c, cols],
                                                 start=False, stop=(c == KC - 1 and j == 2), skip_group_check=True)
                    last.then_inc(u_full, 1)

                def shift(l, g):
                    n = it * INST + (l * PAIR + g)
                    pe.wait_ge(shift_ready, n + 1)
                    pe.matmul(ubank[g][:, :], lhsT=ones[:, :], rhs=flat(SH[:, :, :]), start=False, stop=True,
                              skip_group_check=True).then_inc(u_shifted, 1)

                def row_sums(l, g):
                    pe.wait_ge(e_done, it * INST + (l * PAIR + g + 1))
                    for t in range(GT):
                        last = pe.matmul(ubank[g][:, 2 * t:2 * t + 2], lhsT=E[:, t, :], rhs=ones2[:, :], start=True, stop=True)
                    last.then_inc(z_full, 1)

                def project(l, g, t):
                    for m in (UPPER, LOWER, SELF):
                        p = job["R", l, g, (t, m)]
                        free(p)
                        for c in range(KC):
                            for j, (a, b) in enumerate(TERMS):
                                last = pe.matmul(bank[p % RING][:, 0:D], lhsT=HT[g][a][:, c, t * P:(t + 1) * P],
                                                 rhs=W[l][m][b][:, c, :], start=(c == 0 and j == 0), stop=(c == KC - 1 and j == 2))
                        last.then_inc(bank_full, 1)

                def combine(l, g):
                    n = it * INST + (l * PAIR + g)
                    pe.wait_ge(p_lo, n + 2)
                    for t in range(GT):
                        p = job["C", l, g, t]
                        free(p)
                        pe.wait_ge(hl_lo, n * (2 * GT) + (2 * t + 2 + SLOTS))
                        for side in (UPPER, LOWER):
                            for j, (a, b) in enumerate(TERMS):
                                last = pe.matmul(bank[p % RING][:, 0:HLW], lhsT=PR[a][:, side, t, :], rhs=HL[b][:, side, t, :],
                                                 start=(side == UPPER and j == 0), stop=(side == LOWER and j == 2))
                        last.then_inc(bank_full, 1)

                def projections(l, g):
                    project(l, g, 0)
                    shift(l, g)
                    project(l, g, 1)
                    project(l, g, 2)
                    row_sums(l, g)
                    project(l, g, 3)

                for l in range(LAYERS):
                    head(l, 0)
                    scores(l, 0)
                    projections(l, 0)
                    head(l, 1)
                    scores(l, 1)
                    combine(l, 0)
                    projections(l, 1)
                    combine(l, 1)

        @block.scalar
        def _(act):
            act.wait_ge(made, MADE)
            act.activation(identr[:, :], ident[:, :], ACT.Copy).then_inc(identr_made, 1)
            for m, (_, l, kind) in enumerate(mats):
                act.wait_ge(w_t, m + 1)
                for c in range(KC):
                    last = act.activation(W[l][kind][0][:, c, :], bank[m % 2 * KC + c][:, 0:D], ACT.Copy)
                last.then_inc(w_hi, 1)

            with act.Fori(0, STEPS, 1) as it:
                def split_t(l, g):
                    for c in range(KC):
                        p = job["T", l, g, c]
                        act.wait_ge(bank_full, it * JOBS + (p + 1))
                        act.activation(HT[g][0][:, c, :], bank[p % RING][:, :], ACT.Relu if l else ACT.Copy).then_inc(ht_hi, 1)

                def exps(l, g):
                    n = it * INST + (l * PAIR + g)
                    act.wait_ge(es_done, n + 1)
                    act.wait_ge(u_shifted, n + 1)
                    act.activation(flat(E[:, :, :]), ubank[g][:, :], ACT.Exp, scale=TEMPER).then_inc(e_done, 1)

                def split_r(l, g, t):
                    for m in (UPPER, LOWER):
                        act.wait_ge(drained, it * JOBS + (job["R", l, g, (t, m)] + 1 + CREDIT))
                        act.activation(HL[0][:, m, t, 0:D], HB[:, (2 * t + m) % SLOTS, :], ACT.Copy).then_inc(hl_hi, 1)

                def split_p(l, g):
                    act.wait_ge(em_done, it * INST + (l * PAIR + g + 2))
                    act.activation(PR[0][:, :, :, :], EM[:, :, :, :], ACT.Copy).then_inc(p_hi, 1)

                for l in range(LAYERS):
                    for g in range(PAIR):
                        split_t(l, g)
                        split_r(l, g, 0)
                        exps(l, g)
                        split_r(l, g, 1)
                        split_r(l, g, 2)
                        split_p(l, g)
                        split_r(l, g, 3)

        @block.gpsimd
        def _(pool):
            identity(pool, ident, zeroed, made)
            for g in range(PAIR):
                pool.memset(A[g][:, :, :], 0.0).then_inc(made, 1)
            pool.memset(as_f32(ones[:, :]), 1.0)
            pool.memset(ones2[:, :], 1.0).then_inc(p_lo, 1)
            pool.memset(scratch2[:, :, :], 0.0).then_inc(es_done, 1)
            pool.memset(mhalf[:, :], -0.5).then_inc(made, 1)
            pool.wait_ge(made, MADE)
            pool.memset(as_f32(HL[1][:, :, :, D:HLW]), 0.0)
            pool.memset(as_f32(HL[0][:, :, :, D:HLW]), 1.0).then_inc(hl_lo, SLOTS)

            with pool.Fori(0, STEPS, 1) as it:
                def carry_wait(k):
                    pool.tensor_tensor(scratch2[:, k, :], mhalf[:, :], mhalf[:, :], ALU.mult)

                def masks(g):
                    pool.wait_ge(em_done, it * INST + 1)
                    pool.wait_ge(drained, it * JOBS + (job["A", 0, g, 0] + 1 + CREDIT))
                    carry_wait(g)
                    for m, (op, sign) in enumerate(((ALU.is_gt, 1), (ALU.is_gt, -1), (ALU.is_equal, 1))):
                        ins = pool.affine_select(out=AM[g][:, m], in_=AT[:, :, :], compare_op=op, fill=0.0, base=0,
                                                 pattern=[[0, GT], [-sign, P]], channel_multiplier=sign)
                    ins.then_inc(a_free[g], 1)

                def split_r(l, g, t):
                    n = it * INST + (l * PAIR + g)
                    for m in (UPPER, LOWER):
                        pool.wait_ge(hl_hi, n * (2 * GT) + (2 * t + m + 1))
                        pool.tensor_tensor(HL[1][:, m, t, 0:D], HB[:, (2 * t + m) % SLOTS, :], as_f32(HL[0][:, m, t, 0:D]),
                                           ALU.subtract).then_inc(hl_lo, 1)

                def diagonal(l, g):
                    n = it * INST + (l * PAIR + g)
                    if l == 0:
                        pool.wait_ge(a_free[g], it + 1)
                    pool.wait_ge(dg_done, n + 1)
                    pool.wait_ge(e_done, n + 1)
                    pool.tensor_tensor(ES[:, :, :], E[:, :, :], AM[g][:, 2], ALU.mult).then_inc(es_done, 1)

                def split_p(l, g):
                    pool.wait_ge(p_hi, it * INST + (l * PAIR + g + 1))
                    pool.tensor_tensor(PR[1][:, :, :, :].rearrange("p s t i -> p (s t i)"), EM[:, :, :, :].rearrange("p s t i -> p (s t i)"),
                                       as_f32(PR[0][:, :, :, :]).rearrange("p s t i -> p (s t i)"), ALU.subtract).then_inc(p_lo, 1)

                def deviation(l, g):
                    pool.wait_ge(var_ready, it * INST + (l * PAIR + g + 1))
                    pool.tensor_tensor(FC[:, :], VV[:, :], mhalf[:, :], ALU.pow).then_inc(sd_ready, 1)

                def final_deviation(g):
                    pool.wait_ge(var2_ready, it * PAIR + (g + 1))
                    pool.tensor_tensor(RS[:, :], VE[:, :], mhalf[:, :], ALU.pow).then_inc(rs_ready, 1)

                for l in range(LAYERS):
                    for g in range(PAIR):
                        if l == 0:
                            masks(g)
                        if g == 1:
                            deviation(l, 0)
                        split_r(l, g, 0)
                        if g == 1 and l == LAYERS - 1:
                            final_deviation(0)
                        split_r(l, g, 1)
                        diagonal(l, g)
                        split_r(l, g, 2)
                        split_p(l, g)
                        split_r(l, g, 3)
                    deviation(l, 1)
                    if l == LAYERS - 1:
                        final_deviation(1)

        V_STEPS = INST * (1 + 3 * GT + 2) + PAIR * (4 * GT - 1)

        @block.vector
        def _(dve):
            dve.memset(as_f32(cross[:, :, :]), 0.0).then_inc(cross_made, 1)
            dve.wait_ge(cross_made, 1)
            dve.memset(as_f32(cross[0:NODES, :, NODES:P]), CROSS)
            dve.memset(as_f32(cross[NODES:P, :, 0:NODES]), CROSS).then_inc(cross_made, 1)
            for m, (_, l, kind) in enumerate(mats):
                dve.wait_ge(w_hi, m + 1)
                for c in range(KC):
                    last = dve.tensor_tensor(W[l][kind][1][:, c, :], bank[m % 2 * KC + c][:, 0:D], as_f32(W[l][kind][0][:, c, :]), ALU.subtract)
                last.then_inc(w_lo, 1)
            dve.wait_ge(c_in, 16 * 5 * LAYERS)
            dve.wait_ge(made, MADE)
            dve.memset(scratch[:, 0:1], 0.0).then_inc(drained, CREDIT)
            dve.memset(scratch[:, 1:2], 0.0).then_inc(z_read, PAIR)
            for g in range(PAIR):
                dve.memset(scratch[:, 2 + g:3 + g], 0.0).then_inc(stored[g], 16)
            dve.memset(scratch[:, 4:5], 0.0).then_inc(dg_done, 1)
            dve.memset(scratch[:, 5:6], 0.0).then_inc(em_done, 1)

            with dve.Fori(0, STEPS, 1) as it:
                count = [0]

                def step(ins):
                    count[0] += 1
                    ins.then_inc(v_done, 1)
                    return count[0]

                def own(k):
                    dve.wait_ge(v_done, it * V_STEPS + k)

                def full(*name):
                    p = job[name]
                    dve.wait_ge(bank_full, it * JOBS + (p + 1))
                    return bank[p % RING]

                def masks(g):
                    if g == 0:
                        dve.wait_ge(em_done, it * INST + 1)
                    else:
                        dve.wait_ge(a_free[0], it + 1)
                    dve.tensor_copy(flat(AT[:, :, :]), full("A", 0, g, 0)[:, :]).then_inc(drained, 1)

                def split_t(l, g):
                    for c in range(KC):
                        ps = full("T", l, g, c)
                        dve.wait_ge(ht_hi, (it * INST + (l * PAIR + g)) * KC + (c + 1))
                        hi, lo = as_f32(HT[g][0][:, c, :]), HT[g][1][:, c, :]
                        if l == 0:
                            dve.tensor_tensor(lo, ps[:, :], hi, ALU.subtract).then_inc(drained, 1)
                        else:
                            dve.scalar_tensor_tensor(lo, ps[:, :], 0.0, hi, ALU.max, ALU.subtract).then_inc(drained, 1)

                def maxima(l, g):
                    n = it * INST + (l * PAIR + g)
                    dve.wait_ge(u_full, n + 1)
                    k = step(dve.tensor_reduce(MX[:, :], ubank[g][:, :].rearrange("p (t i) -> p t i", t=GT), AX.X, ALU.max))
                    own(k)
                    for t in range(GT):
                        ins = dve.tensor_scalar(SH[:, t, :], ident[:, :], MX[:, t:t + 1], -1.0, ALU.mult, ALU.mult)
                    ins.then_inc(shift_ready, 1)

                def add_bias(l, g, t):
                    n = it * INST + (l * PAIR + g)
                    for m in (UPPER, LOWER, SELF):
                        ps = full("R", l, g, (t, m))
                        if m == SELF:
                            dst = HS[:, t, :]
                        else:
                            dve.wait_ge(hl_lo, n * (2 * GT) + (2 * t + m + 1))
                            dst = HB[:, (2 * t + m) % SLOTS, :]
                        dve.tensor_tensor(dst, ps[:, 0:D], bias[:, l, m], ALU.add).then_inc(drained, 1)

                def mask_exp(l, g):
                    n = it * INST + (l * PAIR + g)
                    if l == 0:
                        dve.wait_ge(a_free[g], it + 1)
                    dve.wait_ge(p_lo, n + 1)
                    dve.wait_ge(e_done, n + 1)
                    for side in (UPPER, LOWER):
                        ins = dve.tensor_tensor(EM[:, side], E[:, :, :], AM[g][:, side], ALU.mult)
                    ins.then_inc(em_done, 1)

                def diagonal(l, g):
                    dve.wait_ge(es_done, it * INST + (l * PAIR + g + 2))
                    dve.tensor_reduce(DG[:, :], ES[:, :, :], AX.X, ALU.add).then_inc(dg_done, 1)

                def statistics(l, g):
                    n = it * INST + (l * PAIR + g)
                    dve.wait_ge(dg_done, n + 2)
                    if l == 0:
                        dve.wait_ge(stored[g], it * 16 + 16)
                    for t0 in range(0, GT, 2):
                        pair = (t0, t0 + 1)
                        s = {}
                        for t in pair:
                            ps = full("C", l, g, t)
                            s[t] = step(dve.tensor_scalar(SS[:, t:t + 1], ps[:, D:D + 1], DG[:, t:t + 1], None, ALU.add))
                            dve.scalar_tensor_tensor(O[g][:, t, :], HS[:, t, :], DG[:, t:t + 1], ps[:, 0:D],
                                                     ALU.mult, ALU.add).then_inc(drained, 1)
                        for t in pair:
                            dve.wait_ge(drained, it * JOBS + (job["C", l, g, t] + 1 + CREDIT))
                            s[t] = step(dve.bn_stats(ST[:, t, :], O[g][:, t, :]))
                        own(s[t0 + 1])
                        dve.tensor_scalar(scratch[:, 6 + t0 // 2:7 + t0 // 2], DG[:, 0:1], 0.0, None, ALU.mult)
                        for t in pair:
                            s[t] = step(dve.bn_aggr(MV[:, t, :], ST[:, t, :]))
                        for t in pair:
                            own(s[t])
                            ins = dve.scalar_tensor_tensor(O[g][:, t, :], O[g][:, t, :], MV[:, t, 0:1], gain[:, l, :],
                                                           ALU.subtract, ALU.mult)
                    mean_out = step(ins)
                    dve.wait_ge(z_full, n + 1)
                    dve.scalar_tensor_tensor(DEN[:, :], ubank[g][:, 0:2 * GT:2], 1e-10, SS[:, :], ALU.mult, ALU.add).then_inc(z_read, 1)
                    dve.wait_ge(z_read, n + 1 + PAIR)
                    k = step(dve.tensor_tensor(D2[:, :], DEN[:, :], DEN[:, :], ALU.mult))
                    own(k)
                    dve.scalar_tensor_tensor(VV[:, :], D2[:, :], 1e-12, MV[:, :, 1], ALU.mult, ALU.add).then_inc(var_ready, 1)
                    return mean_out

                def finish(l, g, mean_out):
                    dve.wait_ge(sd_ready, it * INST + (l * PAIR + g + 1))
                    own(mean_out)
                    s = {}
                    for t in range(GT):
                        ins = dve.scalar_tensor_tensor(O[g][:, t, :], O[g][:, t, :], FC[:, t:t + 1], beta[:, l, :], ALU.mult, ALU.add)
                        if l == LAYERS - 1:
                            s[t] = step(ins)
                    if l < LAYERS - 1:
                        ins.then_inc(o_ready, 1)
                        return
                    for t in range(GT):
                        own(s[t])
                        s[t] = step(dve.scalar_tensor_tensor(O[g][:, t, :], O[g][:, t, :], 0.0, X[g][:, t, :], ALU.max, ALU.add))
                    for t in range(GT):
                        own(s[t])
                        ins = dve.bn_stats(ST2[:, t, :], O[g][:, t, :])
                        if t == GT - 1:
                            ins.then_inc(x_free[g], 1)
                        else:
                            s[t] = step(ins)
                    dve.wait_ge(x_free[g], it + 1)
                    dve.tensor_scalar(scratch[:, 4 + g:5 + g], FC[:, 0:1], 0.0, None, ALU.mult)
                    for t in range(GT):
                        s[t] = step(dve.bn_aggr(MV2[:, t, :], ST2[:, t, :]))
                    own(s[GT - 1])
                    dve.tensor_scalar(VE[:, :], MV2[:, :, 1], 1e-5, None, ALU.add).then_inc(var2_ready, 1)

                def normalise(g):
                    dve.wait_ge(rs_ready, it * PAIR + (g + 1))
                    for t in range(GT):
                        ins = dve.tensor_scalar(O[g][:, t, :], O[g][:, t, :], MV2[:, t, 0:1], RS[:, t:t + 1], ALU.subtract, ALU.mult)
                    ins.then_inc(o_out, 1)

                for l in range(LAYERS):
                    for g in range(PAIR):
                        if l == 0:
                            masks(g)
                        split_t(l, g)
                        maxima(l, g)
                        if g == 1:
                            mean_out = statistics(l, 0)
                        add_bias(l, g, 0)
                        if g == 1:
                            finish(l, 0, mean_out)
                        add_bias(l, g, 1)
                        mask_exp(l, g)
                        if g == 1 and l == LAYERS - 1:
                            normalise(0)
                        add_bias(l, g, 2)
                        add_bias(l, g, 3)
                        diagonal(l, g)
                    finish(l, 1, statistics(l, 1))
                    if l == LAYERS - 1:
                        normalise(1)
                assert count[0] == V_STEPS, (count[0], V_STEPS)


NAMES = ["x", "adj", "L0_gnn_W_left", "L0_gnn_W_right", "L0_gnn_W_lin", "L0_gnn_b_lin", "L0_gnn_ln_a", "L0_gnn_ln_b",
         "L1_gnn_Wl", "L1_gnn_bl", "L1_gnn_Ws", "L1_gnn_bs", "L1_gnn_Wr", "L1_gnn_br", "L1_gnn_ln_w", "L1_gnn_ln_b"]


def program(nc, a, x1, out):
    network0(nc, a["x"], a["adj"], a["L0_gnn_W_left"], a["L0_gnn_W_right"], a["L0_gnn_W_lin"],
             a["L0_gnn_b_lin"], a["L0_gnn_ln_a"], a["L0_gnn_ln_b"], x1)
    network1(nc, x1, a["adj"], a["L1_gnn_Wl"], a["L1_gnn_bl"], a["L1_gnn_Ws"], a["L1_gnn_bs"],
             a["L1_gnn_Wr"], a["L1_gnn_br"], a["L1_gnn_ln_w"], a["L1_gnn_ln_b"], out)


def kernel(**inputs):
    import concourse.bacc as bacc
    from concourse.bass_utils import run_bass_kernel_spmd as run
    nc = bacc.Bacc("TRN2", target_bir_lowering=False, num_devices=1)
    arrays, aps = {}, {}
    for name in NAMES:
        v = np.ascontiguousarray(inputs[name])
        if name == "x":
            v = v.reshape(GRAPHS * NODES, D)
        arrays["in_" + name] = v
        aps[name] = nc.dram_tensor("in_" + name, v.shape, F32, kind="ExternalInput").ap()
    x1 = nc.dram_tensor("x1", (GRAPHS * NODES, D), F32, kind="Internal").ap()
    out = nc.dram_tensor("out", (GRAPHS * NODES, D), F32, kind="ExternalOutput").ap()
    program(nc, aps, x1, out)
    r = run(nc, [arrays], core_ids=[0])
    return r.results[0]["out"].reshape(GRAPHS, NODES, D)
```

```python
import numpy as np
import concourse.bass as bass
from concourse import mybir
from contextlib import ExitStack

F32 = mybir.dt.float32
F32R = mybir.dt.float32r
ALU = mybir.AluOpType
ACT = mybir.ActivationFunctionType
AX = mybir.AxisListType

GRAPHS, NODES, D = 128, 64, 384
LAYERS = 2
P = 128
KC = D // P
GT = 4
GROUPS = GRAPHS * NODES // (GT * P)
PAIR = 2
STEPS = GROUPS // PAIR
INST = LAYERS * PAIR
RING = 6
CREDIT = RING
HLW = D + 2
TEMPER = 1.0 / float(np.sqrt(D))
CROSS = -float(2.0 ** 100)
TERMS = ((0, 0), (0, 1), (1, 0))


class Plan:

    def __init__(self, body, last, head):
        self.jobs, self.body, self.last = len(body), body, last
        self.ahead = body.index(head[0])
        self.behind = len(body) - self.ahead - len(head)
        assert body[self.ahead:self.ahead + len(head)] == head
        self.bank_of = {name: p % RING for p, name in enumerate(body)}
        self.need = {}
        for which, steps in (("body", (body, body)), ("last", (body, last))):
            user, n = {}, 0
            for step in steps:
                for name in step:
                    self.need[which, name] = user.get(self.bank_of[name], -len(body)) - len(body) + 1 + CREDIT
                    user[self.bank_of[name]] = n
                    n += 1

    def done(self, name, step):
        order = self.last if isinstance(step, int) and step == STEPS - 1 else self.body
        return (step + 1) * self.jobs + (order.index(name) + 1)

    def drained(self, name, step):
        return self.done(name, step) + CREDIT

    def free(self, name, step):
        which = "last" if isinstance(step, int) and step == STEPS - 1 else "body"
        return (step + 1) * self.jobs + self.need[which, name]


def following(k):
    return divmod((k + 1) % INST, PAIR)


def as_f32(ap):
    return ap.bitcast(F32)


def flat(ap):
    return ap.rearrange("p t i -> p (t i)")


def identity(pool, ident, zeroed, made):
    pool.memset(ident[:, :], 0.0).then_inc(zeroed, 1)
    pool.wait_ge(zeroed, 1)
    pool.affine_select(out=ident[:, :], in_=ident[:, :], compare_op=ALU.not_equal, fill=1.0, base=0,
                       pattern=[[-1, P]], channel_multiplier=1).then_inc(made, 1)


def network0(nc, x, adj, w_left, w_right, w_lin, b_lin, ln_a, ln_b, out):
    def plan(last):
        order = []
        for k in range(INST):
            l, g = divmod(k, PAIR)
            pl, pg = divmod(k - 1, PAIR)
            nl, ng = following(k)
            head = [("A", nl, ng, 0)] if nl == 0 else []
            head += [("T", nl, ng, c) for c in range(KC)]
            order += [("N", l, g, i) for i in range(KC)]
            order += [("C", pl, pg, t) for t in range(GT)] if k else []
            order += [("N", l, g, i) for i in range(KC, 2 * KC)]
            order += [("H", l, g, t) for t in range(GT - 1)]
            if k < INST - 1:
                order += head + [("H", l, g, GT - 1)]
            else:
                order += [("H", l, g, GT - 1)] + ([] if last else head) + [("C", l, g, t) for t in range(GT)]
        return order

    HEAD = [("A", 0, 0, 0)] + [("T", 0, 0, c) for c in range(KC)]
    jobs = Plan(plan(False), plan(True), HEAD)
    SLOTS = 4

    ctx = ExitStack()
    with ctx:
        def sb(name, shape, dt=F32):
            return ctx.enter_context(nc.sbuf_tensor("n0_" + name, shape, dt))

        def sem(name):
            return ctx.enter_context(nc.semaphore("n0_" + name))

        ident = sb("ident", [P, P])
        W = [[[sb(f"w{l}{m}{s}", [P, KC, D], F32R) for s in range(2)] for m in range(3)] for l in range(LAYERS)]
        bias, gain, beta = (sb(n, [P, LAYERS, D]) for n in ("bias", "gain", "beta"))
        X = [sb(f"x{g}", [P, GT, D]) for g in range(PAIR)]
        O = [sb(f"o{g}", [P, GT, D]) for g in range(PAIR)]
        stage = [X[1], O[1]]
        A = [sb(f"a{g}", [P, GT, P]) for g in range(PAIR)]
        AT = [sb(f"at{g}", [P, GT, P]) for g in range(PAIR)]
        SM = [sb(f"sm{g}", [P, GT, 2, P]) for g in range(PAIR)]
        HT = [[sb(f"ht{g}{s}", [P, KC, GT * P], F32R) for s in range(2)] for g in range(PAIR)]
        N = [sb(f"n{s}", [P, KC, 2, GT * P], F32R) for s in range(2)]
        HB = sb("hb", [P, SLOTS, D])
        HL = [sb(f"hl{s}", [P, GT, HLW], F32R) for s in range(2)]
        UM = [sb(f"um{k}", [P, 2, 2, P]) for k in range(2)]
        E = sb("e", [P, GT, P])
        PR = [sb(f"p{s}", [P, GT, P], F32R) for s in range(2)]
        half, mhalf = sb("half", [P, GT]), sb("mhalf", [P, GT])
        ST, MV = sb("st", [P, GT, 6]), sb("mv", [P, GT, 2])
        WS, SD, FC = sb("ws", [P, GT]), sb("sd", [P, GT]), sb("fc", [P, GT])
        ST2, MV2, VE = sb("st2", [P, GT, 6]), sb("mv2", [P, GT, 2]), sb("ve", [P, GT])
        RS, NB = ([sb(f"{n}{g}", [P, GT]) for g in range(PAIR)] for n in ("rs", "nb"))
        scratch, scratch2 = sb("scratch", [P, 8]), sb("scratch2", [P, 4, GT])

        bank = [ctx.enter_context(nc.psum_tensor(f"n0_bank{i}", [P, 512], F32)) for i in range(RING)]
        ubank = [ctx.enter_context(nc.psum_tensor(f"n0_u{i}", [P, 512], F32)) for i in range(2)]

        bank_full = sem("bank_full")
        drained = sem("drained")
        x_in, a_in, x_free, a_free, stored = (
            [sem(f"{n}{g}") for g in range(PAIR)] for n in ("x_in", "a_in", "x_free", "a_free", "stored"))
        ht_hi, n_hi = sem("ht_hi"), sem("n_hi")
        u_full, u_masked, u_added = sem("u_full"), sem("u_masked"), sem("u_added")
        e_done, p_done, p_hi, p_lo = sem("e_done"), sem("p_done"), sem("p_hi"), sem("p_lo")
        hl_hi, hl_lo = sem("hl_hi"), sem("hl_lo")
        var_ready, sd_ready, o_ready, var2_ready, rs_ready, nb_ready, o_out = (
            sem(n) for n in ("var_ready", "sd_ready", "o_ready", "var2_ready", "rs_ready", "nb_ready", "o_out"))
        v_done = sem("v_done")
        w_in = [sem("w_in0"), sem("w_in1")]
        c_in, w_hi, w_lo, w_t, zeroed, made = (sem(n) for n in ("c_in", "w_hi", "w_lo", "w_t", "zeroed", "made"))
        MADE = 4

        xg = x.rearrange("(g t p) d -> g p t d", p=P, t=GT)
        og = out.rearrange("(g t p) d -> g p t d", p=P, t=GT)
        ag = adj.rearrange("(g t q) j i -> g q j t i", q=2, t=GT)
        mats = [(w, l, m) for l in range(LAYERS) for m, w in enumerate((w_left[l], w_right[l], w_lin[l]))]
        TRANSPOSED = 2

        block = ctx.enter_context(nc.Block())

        @block.sync
        def _(sp):
            def weight(m):
                sp.dma_start(stage[m % 2][:, 0:KC, :], mats[m][0].rearrange("(k p) h -> p k h", p=P)).then_inc(w_in[m % 2], 16)

            def load(step, g, first=False):
                if not first:
                    sp.wait_ge(x_free[g], step)
                sp.dma_start(X[g][:, :, :], xg[step * PAIR + g]).then_inc(x_in[g], 16)
                if not first:
                    sp.wait_ge(a_free[g], step)
                for q in range(2):
                    sp.dma_start(A[g][q * NODES:(q + 1) * NODES, :, q * NODES:(q + 1) * NODES],
                                 ag[step * PAIR + g][q]).then_inc(a_in[g], 16)

            def store(step, g):
                sp.wait_ge(o_out, step * PAIR + g + 1)
                sp.dma_start(og[step * PAIR + g], O[g][:, :, :]).then_inc(stored[g], 16)

            weight(0)
            weight(1)
            for l in range(LAYERS):
                for dst, src in ((bias, b_lin), (gain, ln_a), (beta, ln_b)):
                    sp.dma_start(dst[:, l], src[l].partition_broadcast(P)).then_inc(c_in, 16)
            sp.wait_ge(made, MADE)
            load(0, 0, first=True)
            for m in range(2, len(mats)):
                sp.wait_ge(w_lo, m - 1)
                weight(m)
            sp.wait_ge(w_lo, len(mats))
            load(0, 1, first=True)
            with sp.Fori(0, STEPS - 1, 1) as it:
                for g in range(PAIR):
                    load(it + 1, g)
                    store(it, g)
            for g in range(PAIR):
                store(STEPS - 1, g)
            for g in range(PAIR):
                sp.wait_ge(stored[g], (STEPS + 1) * 16)

        @block.tensor
        def _(pe):
            pe.wait_ge(made, MADE)
            for m, (_, l, kind) in enumerate(mats):
                if kind == TRANSPOSED:
                    pe.wait_ge(w_in[m % 2], 16 * (m // 2 + 1))
                    pe.wait_ge(w_lo, m - 1)
                    for c in range(KC):
                        for k in range(KC):
                            last = pe.transpose(bank[c][:, k * P:(k + 1) * P], stage[m % 2][:, k, c * P:(c + 1) * P], ident[:, :])
                    last.then_inc(w_t, 1)
            pe.wait_ge(w_lo, len(mats))
            pe.wait_ge(bank_full, jobs.ahead)

            def start(name, it):
                pe.wait_ge(drained, jobs.free(name, it))
                return bank[jobs.bank_of[name]]

            def head(it, l, g):
                if l == 0:
                    pe.wait_ge(a_in[g], (it + 1) * 32)
                    ps = start(("A", l, g, 0), it - (g == 0))
                    for t in range(GT):
                        last = pe.transpose(ps[:, t * P:(t + 1) * P], A[g][:, t, :], ident[:, :])
                    last.then_inc(bank_full, 1)
                    pe.wait_ge(x_in[g], (it + 1) * 16)
                else:
                    pe.wait_ge(o_ready, it * PAIR + g + 1)
                src = X[g] if l == 0 else O[g]
                for c in range(KC):
                    ps = start(("T", l, g, c), it - (l == 0 and g == 0))
                    for t in range(GT):
                        last = pe.transpose(ps[:, t * P:(t + 1) * P], src[:, t, c * P:(c + 1) * P], ident[:, :])
                    before_loop = isinstance(it, int) and it == 0 and l == 0 and g == 0 and c == KC - 1
                    last.then_inc(bank_full, 1 + jobs.behind if before_loop else 1)

            def project_scores(it, l, g, i):
                side, c = i // KC, i % KC
                ps = start(("N", l, g, i), it)
                for k in range(KC):
                    if i == 0:
                        pe.wait_ge(drained, jobs.drained(("T", l, g, k), it - (l == 0 and g == 0)))
                    for j, (a, b) in enumerate(TERMS):
                        last = pe.matmul(ps[:, :], lhsT=W[l][side][a][:, k, c * P:(c + 1) * P],
                                         rhs=HT[g][b][:, k, :], start=(k == 0 and j == 0), stop=(k == KC - 1 and j == 2))
                last.then_inc(bank_full, 1)

            def scores(it, l, g):
                n = it * INST + (l * PAIR + g)
                pe.wait_ge(drained, jobs.drained(("N", l, g, 2 * KC - 1), it))
                for k in range(2):
                    pe.wait_ge(u_masked, n * 2 + (k + 1))
                    for t in range(2):
                        cols = slice((2 * k + t) * P, (2 * k + t + 1) * P)
                        for c in range(KC):
                            for j, (a, b) in enumerate(TERMS):
                                last = pe.matmul(ubank[k][:, t * 2 * P:(t + 1) * 2 * P], lhsT=HT[g][a][:, c, cols],
                                                 rhs=N[b][:, c, :, cols], start=(c == 0 and j == 0), stop=(c == KC - 1 and j == 2))
                    last.then_inc(u_full, 1)

            def project(it, l, g, t):
                ps = start(("H", l, g, t), it)
                for c in range(KC):
                    for j, (a, b) in enumerate(TERMS):
                        last = pe.matmul(ps[:, 0:D], lhsT=HT[g][a][:, c, t * P:(t + 1) * P],
                                         rhs=W[l][2][b][:, c, :], start=(c == 0 and j == 0), stop=(c == KC - 1 and j == 2))
                last.then_inc(bank_full, 1)

            def combine(it, l, g):
                n = it * INST + (l * PAIR + g)
                for t in range(GT):
                    ps = start(("C", l, g, t), it)
                    pe.wait_ge(p_lo, n * 2 + (t // 2 + 1 + 2))
                    pe.wait_ge(hl_lo, n * GT + (t + 1 + SLOTS))
                    for j, (a, b) in enumerate(TERMS):
                        last = pe.matmul(ps[:, 0:HLW], lhsT=PR[a][:, t, :], rhs=HL[b][:, t, :], start=(j == 0), stop=(j == 2))
                    last.then_inc(bank_full, 1)

            def body(it, last=False):
                for k in range(INST):
                    l, g = divmod(k, PAIR)
                    nl, ng = following(k)
                    for i in range(KC):
                        project_scores(it, l, g, i)
                    if k:
                        combine(it, *divmod(k - 1, PAIR))
                    for i in range(KC, 2 * KC):
                        project_scores(it, l, g, i)
                    project(it, l, g, 0)
                    scores(it, l, g)
                    project(it, l, g, 1)
                    project(it, l, g, 2)
                    if k < INST - 1:
                        head(it, nl, ng)
                        project(it, l, g, 3)
                    else:
                        project(it, l, g, 3)
                        if not last:
                            head(it + 1, nl, ng)
                        combine(it, l, g)

            head(0, 0, 0)
            with pe.Fori(0, STEPS - 1, 1) as it:
                body(it)
            body(STEPS - 1, last=True)

        @block.scalar
        def _(act):
            for m, (_, l, kind) in enumerate(mats):
                if kind == TRANSPOSED:
                    act.wait_ge(w_t, l + 1)
                    for c in range(KC):
                        last = act.activation(W[l][kind][0][:, c, :], bank[c][:, 0:D], ACT.Copy)
                else:
                    act.wait_ge(w_in[m % 2], 16 * (m // 2 + 1))
                    last = act.activation(W[l][kind][0][:, :, :], stage[m % 2][:, 0:KC, :], ACT.Copy)
                last.then_inc(w_hi, 1)

            def split_t(it, l, g):
                for c in range(KC):
                    name, step = ("T", l, g, c), it - (l == 0 and g == 0)
                    act.wait_ge(bank_full, jobs.done(name, step))
                    act.activation(HT[g][0][:, c, :], bank[jobs.bank_of[name]][:, :], ACT.Relu if l else ACT.Copy).then_inc(ht_hi, 1)

            def split_n(it, l, g):
                for i in range(2 * KC):
                    name = ("N", l, g, i)
                    act.wait_ge(bank_full, jobs.done(name, it))
                    act.activation(N[0][:, i % KC, i // KC, :], bank[jobs.bank_of[name]][:, :], ACT.Copy).then_inc(n_hi, 1)

            def exps(it, l, g):
                n = it * INST + (l * PAIR + g)
                for k in range(2):
                    act.wait_ge(u_added, n * 2 + (k + 1 + 2))
                    act.activation(E[:, 2 * k:2 * k + 2, :], E[:, 2 * k:2 * k + 2, :], ACT.Exp, scale=TEMPER).then_inc(e_done, 1)

            def split_p(it, l, g):
                n = it * INST + (l * PAIR + g)
                for k in range(2):
                    act.wait_ge(p_done, n * 2 + (k + 1 + 2))
                    act.activation(PR[0][:, 2 * k:2 * k + 2, :], E[:, 2 * k:2 * k + 2, :], ACT.Copy).then_inc(p_hi, 1)

            def split_h(it, l, g, t):
                act.wait_ge(drained, jobs.drained(("H", l, g, t), it))
                act.activation(HL[0][:, t, 0:D], HB[:, t % SLOTS, :], ACT.Copy).then_inc(hl_hi, 1)

            def normalise(it, g):
                act.wait_ge(nb_ready, it * PAIR + (g + 1))
                for t in range(GT):
                    ins = act.activation(O[g][:, t, :], O[g][:, t, :], ACT.Identity, bias=NB[g][:, t:t + 1], scale=RS[g][:, t:t + 1])
                ins.then_inc(o_out, 1)

            def body(it, first=False, last=False):
                for k in range(INST):
                    l, g = divmod(k, PAIR)
                    nl, ng = following(k)
                    split_n(it, l, g)
                    split_h(it, l, g, 0)
                    exps(it, l, g)
                    split_h(it, l, g, 1)
                    split_h(it, l, g, 2)
                    if k < INST - 1:
                        split_t(it, nl, ng)
                        split_p(it, l, g)
                        split_h(it, l, g, 3)
                    else:
                        split_p(it, l, g)
                        split_h(it, l, g, 3)
                        if not last:
                            split_t(it + 1, nl, ng)
                    if k == 0 and not first:
                        normalise(it - 1, 1)
                    if k == INST - 1:
                        normalise(it, 0)

            split_t(0, 0, 0)
            body(0, first=True)
            with act.Fori(1, STEPS - 1, 1) as it:
                body(it)
            body(STEPS - 1, last=True)
            normalise(STEPS - 1, 1)

        @block.gpsimd
        def _(pool):
            identity(pool, ident, zeroed, made)
            for g in range(PAIR):
                pool.memset(A[g][:, :, :], 0.0).then_inc(made, 1)
            pool.memset(half[:, :], 0.5).then_inc(p_done, 2)
            pool.memset(scratch2[:, :, :], 0.0).then_inc(u_added, 2)
            pool.memset(mhalf[:, :], -0.5).then_inc(made, 1)
            pool.wait_ge(made, MADE)
            pool.memset(as_f32(HL[1][:, :, D:HLW]), 0.0).then_inc(p_lo, 2)
            pool.memset(as_f32(HL[0][:, :, D:HLW]), 1.0).then_inc(hl_lo, SLOTS)

            def carry_wait(k):
                pool.tensor_tensor(scratch2[:, k, :], half[:, :], half[:, :], ALU.mult)

            def masks(it, g):
                first = isinstance(it, int) and it == 0 and g == 0
                if not first:
                    pool.wait_ge(u_masked, it * (2 * INST) + (2 * (PAIR + g + 1 - INST) + 2))
                pool.wait_ge(drained, jobs.drained(("A", 0, g, 0), it - (g == 0)))
                carry_wait(g)
                pool.affine_select(out=SM[g][:, :, 1, :], in_=A[g][:, :, :], compare_op=ALU.is_gt, fill=0.0, base=0,
                                   pattern=[[0, GT], [1, P]], channel_multiplier=-1)
                pool.affine_select(out=SM[g][:, :, 0, :], in_=AT[g][:, :, :], compare_op=ALU.is_ge, fill=0.0, base=0,
                                   pattern=[[0, GT], [-1, P]], channel_multiplier=1).then_inc(a_free[g], 1)

            def add_scores(it, l, g):
                n = it * INST + (l * PAIR + g)
                pool.wait_ge(p_lo, n * 2 + 2)
                for k in range(2):
                    pool.wait_ge(u_masked, n * 2 + (k + 1 + 2))
                    pool.tensor_tensor(E[:, 2 * k:2 * k + 2, :], UM[k][:, :, 0, :], UM[k][:, :, 1, :], ALU.add).then_inc(u_added, 1)

            def mask_exp(it, l, g):
                n = it * INST + (l * PAIR + g)
                for k in range(2):
                    pool.wait_ge(e_done, n * 2 + (k + 1))
                    pool.tensor_tensor(E[:, 2 * k:2 * k + 2, :], E[:, 2 * k:2 * k + 2, :], AT[g][:, 2 * k:2 * k + 2, :],
                                       ALU.mult).then_inc(p_done, 1)

            def split_p(it, l, g):
                n = it * INST + (l * PAIR + g)
                for k in range(2):
                    pool.wait_ge(p_hi, n * 2 + (k + 1))
                    pool.tensor_tensor(PR[1][:, 2 * k:2 * k + 2, :], E[:, 2 * k:2 * k + 2, :],
                                       as_f32(PR[0][:, 2 * k:2 * k + 2, :]), ALU.subtract).then_inc(p_lo, 1)

            def split_h(it, l, g, t):
                pool.wait_ge(hl_hi, (it * INST + (l * PAIR + g)) * GT + (t + 1))
                pool.tensor_tensor(HL[1][:, t, 0:D], HB[:, t % SLOTS, :], as_f32(HL[0][:, t, 0:D]), ALU.subtract).then_inc(hl_lo, 1)

            def deviation(it, l, g):
                pool.wait_ge(var_ready, it * INST + (l * PAIR + g + 1))
                pool.tensor_tensor(SD[:, :], MV[:, :, 1], half[:, :], ALU.pow).then_inc(sd_ready, 1)

            def final_deviation(it, g):
                pool.wait_ge(var2_ready, it * PAIR + (g + 1))
                pool.tensor_tensor(RS[g][:, :], VE[:, :], mhalf[:, :], ALU.pow).then_inc(rs_ready, 1)

            def body(it, first=False, last=False):
                for k in range(INST):
                    l, g = divmod(k, PAIR)
                    nl, ng = following(k)
                    if k:
                        deviation(it, *divmod(k - 1, PAIR))
                    split_h(it, l, g, 0)
                    if k == INST - 1:
                        final_deviation(it, 0)
                    elif k == 0 and not first:
                        final_deviation(it - 1, 1)
                    add_scores(it, l, g)
                    split_h(it, l, g, 1)
                    mask_exp(it, l, g)
                    split_h(it, l, g, 2)
                    split_p(it, l, g)
                    if k == 0:
                        masks(it, 1)
                    split_h(it, l, g, 3)
                    if k == INST - 1:
                        if not last:
                            masks(it + 1, 0)
                        deviation(it, l, g)

            masks(0, 0)
            body(0, first=True)
            with pool.Fori(1, STEPS - 1, 1) as it:
                body(it)
            body(STEPS - 1, last=True)
            final_deviation(STEPS - 1, 1)

        V_FINISH, V_RESIDUAL = 2, 4 * GT - 1
        V_STEPS = INST * (3 * GT - 1 + V_FINISH) + PAIR * V_RESIDUAL

        @block.vector
        def _(dve):
            for m, (_, l, kind) in enumerate(mats):
                dve.wait_ge(w_hi, m + 1)
                if kind == TRANSPOSED:
                    for c in range(KC):
                        last = dve.tensor_tensor(W[l][kind][1][:, c, :], bank[c][:, 0:D], as_f32(W[l][kind][0][:, c, :]), ALU.subtract)
                else:
                    last = dve.tensor_tensor(W[l][kind][1][:, :, :], stage[m % 2][:, 0:KC, :], as_f32(W[l][kind][0][:, :, :]), ALU.subtract)
                last.then_inc(w_lo, 1)
            dve.wait_ge(c_in, 16 * 3 * LAYERS)
            dve.memset(scratch[:, 0:1], 0.0).then_inc(drained, CREDIT + jobs.ahead)
            dve.memset(scratch[:, 1:2], 0.0).then_inc(u_masked, 2)
            for g in range(PAIR):
                dve.memset(scratch[:, 2 + g:3 + g], 0.0).then_inc(stored[g], 16)

            dve.memset(scratch[:, 4:5], 0.0).then_inc(v_done, V_FINISH + V_RESIDUAL)
            dve.memset(scratch[:, 5:6], 0.0).then_inc(bank_full, jobs.ahead)
            count = [0]

            def step(ins):
                count[0] += 1
                ins.then_inc(v_done, 1)
                return count[0]

            def own(it, k):
                dve.wait_ge(v_done, it * V_STEPS + k)

            def full(name, it):
                dve.wait_ge(bank_full, jobs.done(name, it))
                return bank[jobs.bank_of[name]]

            def masks(it, g):
                first = isinstance(it, int) and it == 0 and g == 0
                if not first:
                    dve.wait_ge(p_done, it * (2 * INST) + (2 * (PAIR + g + 1 - INST) + 2))
                dve.tensor_copy(flat(AT[g][:, :, :]), full(("A", 0, g, 0), it - (g == 0))[:, :]).then_inc(drained, 1)

            def split_t(it, l, g):
                for c in range(KC):
                    ps = full(("T", l, g, c), it - (l == 0 and g == 0))
                    dve.wait_ge(ht_hi, (it * INST + (l * PAIR + g)) * KC + (c + 1))
                    hi, lo = as_f32(HT[g][0][:, c, :]), HT[g][1][:, c, :]
                    before_loop = isinstance(it, int) and it == 0 and l == 0 and g == 0 and c == KC - 1
                    if l == 0:
                        dve.tensor_tensor(lo, ps[:, :], hi, ALU.subtract).then_inc(drained, 1 + jobs.behind if before_loop else 1)
                    else:
                        dve.scalar_tensor_tensor(lo, ps[:, :], 0.0, hi, ALU.max, ALU.subtract).then_inc(drained, 1)

            def split_n(it, l, g, i):
                ps = full(("N", l, g, i), it)
                dve.wait_ge(n_hi, (it * INST + (l * PAIR + g)) * (2 * KC) + (i + 1))
                dve.tensor_tensor(N[1][:, i % KC, i // KC, :], ps[:, :], as_f32(N[0][:, i % KC, i // KC, :]),
                                  ALU.subtract).then_inc(drained, 1)

            def mask_scores(it, l, g):
                n = it * INST + (l * PAIR + g)
                dve.wait_ge(u_added, n * 2 + 2)
                if l == 0:
                    dve.wait_ge(a_free[g], it + 1)
                for k in range(2):
                    dve.wait_ge(u_full, n * 2 + (k + 1))
                    dve.tensor_tensor(UM[k][:, :, :, :].rearrange("p t s i -> p (t s i)"), ubank[k][:, :],
                                      SM[g][:, 2 * k:2 * k + 2, :, :].rearrange("p t s i -> p (t s i)"),
                                      ALU.mult).then_inc(u_masked, 1)

            def add_bias(it, l, g, t):
                ps = full(("H", l, g, t), it)
                dve.wait_ge(hl_lo, (it * INST + (l * PAIR + g)) * GT + (t + 1))
                dve.tensor_tensor(HB[:, t % SLOTS, :], ps[:, 0:D], bias[:, l, :], ALU.add).then_inc(drained, 1)

            def statistics(it, l, g):
                if l == 0:
                    dve.wait_ge(stored[g], it * 16 + 16)
                for t0 in range(0, GT, 2):
                    pair = (t0, t0 + 1)
                    ps = {t: bank[jobs.bank_of["C", l, g, t]] for t in pair}
                    a = {}
                    for t in pair:
                        s = step(dve.bn_stats(ST[:, t, :], full(("C", l, g, t), it)[:, 0:D]))
                    own(it, s)
                    for t in pair:
                        step(dve.tensor_scalar(WS[:, t:t + 1], ps[t][:, D:D + 1], 1e-10, 1e-3, ALU.add, ALU.mult))
                    for t in pair:
                        ins = dve.bn_aggr(MV[:, t, :], ST[:, t, :])
                        if t == GT - 1:
                            ins.then_inc(var_ready, 1)
                        else:
                            a[t] = step(ins)
                    for t in pair:
                        if t == GT - 1:
                            dve.wait_ge(var_ready, it * INST + (l * PAIR + g + 1))
                        else:
                            own(it, a[t])
                        dve.scalar_tensor_tensor(O[g][:, t, :], ps[t][:, 0:D], MV[:, t, 0:1], gain[:, l, :],
                                                 ALU.subtract, ALU.mult).then_inc(drained, 1)

            def finish(now, it, l, g):
                dve.wait_ge(sd_ready, it * INST + (l * PAIR + g + 1))
                own(now, step(dve.scalar_tensor_tensor(FC[:, :], SD[:, :], float(np.sqrt(D / (D - 1.0))), WS[:, :], ALU.mult, ALU.add)))
                own(now, step(dve.reciprocal(FC[:, :], FC[:, :])))
                dve.wait_ge(drained, jobs.drained(("C", l, g, GT - 1), it))
                s = {}
                for t in range(GT):
                    ins = dve.scalar_tensor_tensor(O[g][:, t, :], O[g][:, t, :], FC[:, t:t + 1], beta[:, l, :], ALU.mult, ALU.add)
                    if l == LAYERS - 1:
                        s[t] = step(ins)
                if l < LAYERS - 1:
                    ins.then_inc(o_ready, 1)
                    return
                for t in range(GT):
                    own(now, s[t])
                    ins = dve.scalar_tensor_tensor(O[g][:, t, :], O[g][:, t, :], 0.0, X[g][:, t, :], ALU.max, ALU.add)
                    if t == GT - 1:
                        ins.then_inc(x_free[g], 1)
                    else:
                        s[t] = step(ins)
                return s

            def final_statistics(now, it, g, s):
                for t in range(GT):
                    if t == GT - 1:
                        dve.wait_ge(x_free[g], it + 1)
                    else:
                        own(now, s[t])
                    s[t] = step(dve.bn_stats(ST2[:, t, :], O[g][:, t, :]))
                own(now, s[GT - 1])
                dve.tensor_scalar(scratch[:, 2 + g:3 + g], FC[:, 0:1], 0.0, None, ALU.mult)
                for t in range(GT):
                    s[t] = step(dve.bn_aggr(MV2[:, t, :], ST2[:, t, :]))
                own(now, s[GT - 1])
                dve.tensor_scalar(VE[:, :], MV2[:, :, 1], 1e-5, None, ALU.add).then_inc(var2_ready, 1)

            def minus_mean(it, g):
                dve.wait_ge(rs_ready, it * PAIR + (g + 1))
                dve.scalar_tensor_tensor(NB[g][:, :], MV2[:, :, 0], -1.0, RS[g][:, :], ALU.mult, ALU.mult).then_inc(nb_ready, 1)

            def body(it, first=False, last=False):
                count[0] = V_FINISH + V_RESIDUAL if first else 0
                for k in range(INST):
                    l, g = divmod(k, PAIR)
                    nl, ng = following(k)
                    ended = {}
                    for i in range(KC):
                        split_n(it, l, g, i)
                    if k:
                        statistics(it, *divmod(k - 1, PAIR))
                    elif not first:
                        ended = finish(it, it - 1, LAYERS - 1, 1)
                    for i in range(KC, 2 * KC):
                        split_n(it, l, g, i)
                    if k:
                        ended = finish(it, it, *divmod(k - 1, PAIR))
                    add_bias(it, l, g, 0)
                    if ended:
                        final_statistics(it, it if k else it - 1, 1 - g, ended)
                    mask_scores(it, l, g)
                    add_bias(it, l, g, 1)
                    if ended:
                        minus_mean(it if k else it - 1, 1 - g)
                    add_bias(it, l, g, 2)
                    if k == INST - 1:
                        add_bias(it, l, g, 3)
                    if not (k == INST - 1 and last):
                        if nl == 0:
                            masks(it + (k == INST - 1), ng)
                        split_t(it + (k == INST - 1), nl, ng)
                    if k < INST - 1:
                        add_bias(it, l, g, 3)
                statistics(it, LAYERS - 1, 1)
                assert count[0] == V_STEPS, (count[0], V_STEPS)

            masks(0, 0)
            split_t(0, 0, 0)
            body(0, first=True)
            with dve.Fori(1, STEPS - 1, 1) as it:
                body(it)
            body(STEPS - 1, last=True)
            count[0] = 0
            ended = finish(STEPS, STEPS - 1, LAYERS - 1, 1)
            final_statistics(STEPS, STEPS - 1, 1, ended)
            minus_mean(STEPS - 1, 1)


def network1(nc, x, adj, w_upper, b_upper, w_self, b_self, w_lower, b_lower, ln_w, ln_b, out):
    UPPER, LOWER, SELF = range(3)
    def plan(last):
        order = []
        for k in range(INST):
            l, g = divmod(k, PAIR)
            nl, ng = following(k)
            head = [("A", nl, ng, 0)] if nl == 0 else []
            head += [("T", nl, ng, c) for c in range(KC)]
            rows = [[("R", l, g, (t, m)) for m in (UPPER, LOWER, SELF)] for t in range(GT)]
            order += rows[0] + rows[1] + rows[2]
            order += [] if last and k == INST - 1 else head
            order += rows[3]
            order += [("C", l, g, t) for t in range(GT)]
        return order

    HEAD = [("A", 0, 0, 0)] + [("T", 0, 0, c) for c in range(KC)]
    jobs = Plan(plan(False), plan(True), HEAD)
    SLOTS = 4

    ctx = ExitStack()
    with ctx:
        def sb(name, shape, dt=F32):
            return ctx.enter_context(nc.sbuf_tensor("n1_" + name, shape, dt))

        def sem(name):
            return ctx.enter_context(nc.semaphore("n1_" + name))

        ident, identr, ones = sb("ident", [P, P]), sb("identr", [P, P], F32R), sb("ones", [P, P], F32R)
        cross = sb("cross", [P, GT, P], F32R)
        W = [[[sb(f"w{l}{m}{s}", [P, KC, D], F32R) for s in range(2)] for m in range(3)] for l in range(LAYERS)]
        bias = sb("bias", [P, LAYERS, 3, D])
        gain, beta = (sb(n, [P, LAYERS, D]) for n in ("gain", "beta"))
        X = [sb(f"x{g}", [P, GT, D]) for g in range(PAIR)]
        O = [sb(f"o{g}", [P, GT, D]) for g in range(PAIR)]
        stage = [X[1], O[1]]
        A = [sb(f"a{g}", [P, GT, P]) for g in range(PAIR)]
        AT = sb("at", [P, GT, P])
        AM = [sb(f"am{g}", [P, 3, GT, P]) for g in range(PAIR)]
        HT = [[sb(f"ht{g}{s}", [P, KC, GT * P], F32R) for s in range(2)] for g in range(PAIR)]
        HB = sb("hb", [P, SLOTS, D])
        HL = [sb(f"hl{s}", [P, 2, GT, HLW], F32R) for s in range(2)]
        HS = sb("hs", [P, GT, D])
        MX, SH = sb("mx", [P, GT]), sb("sh", [P, GT, P], F32R)
        E = sb("e", [P, GT, P])
        EM = sb("em", [P, 2, GT, P])
        ES, DG = sb("es", [P, GT, P]), sb("dg", [P, GT])
        PR = [sb(f"p{s}", [P, 2, GT, P], F32R) for s in range(2)]
        ones2 = sb("ones2", [P, 2])
        mhalf = sb("mhalf", [P, GT])
        ST, MV = sb("st", [P, GT, 6]), sb("mv", [P, GT, 2])
        SS, DEN, D2, VV, FC = (sb(n, [P, GT]) for n in ("ss", "den", "d2", "vv", "fc"))
        ST2, MV2, VE = sb("st2", [P, GT, 6]), sb("mv2", [P, GT, 2]), sb("ve", [P, GT])
        RS, NB = ([sb(f"{n}{g}", [P, GT]) for g in range(PAIR)] for n in ("rs", "nb"))
        scratch, scratch2 = sb("scratch", [P, 12]), sb("scratch2", [P, 4, GT])

        bank = [ctx.enter_context(nc.psum_tensor(f"n1_bank{i}", [P, 512], F32)) for i in range(RING)]
        ubank = [ctx.enter_context(nc.psum_tensor(f"n1_u{i}", [P, 512], F32)) for i in range(PAIR)]

        bank_full = sem("bank_full")
        drained = sem("drained")
        x_in, a_in, x_free, a_free, stored = (
            [sem(f"{n}{g}") for g in range(PAIR)] for n in ("x_in", "a_in", "x_free", "a_free", "stored"))
        ht_hi, u_full, u_shifted, z_full, z_read = (sem(n) for n in ("ht_hi", "u_full", "u_shifted", "z_full", "z_read"))
        shift_ready, e_done, em_done, es_done, dg_done, p_hi, p_lo = (
            sem(n) for n in ("shift_ready", "e_done", "em_done", "es_done", "dg_done", "p_hi", "p_lo"))
        hl_hi, hl_lo = sem("hl_hi"), sem("hl_lo")
        var_ready, sd_ready, o_ready, var2_ready, rs_ready, nb_ready, o_out = (
            sem(n) for n in ("var_ready", "sd_ready", "o_ready", "var2_ready", "rs_ready", "nb_ready", "o_out"))
        mx_done = sem("mx_done")
        v_done = sem("v_done")
        w_in = [sem("w_in0"), sem("w_in1")]
        c_in, w_hi, w_lo, w_t, zeroed, made = (sem(n) for n in ("c_in", "w_hi", "w_lo", "w_t", "zeroed", "made"))
        MADE = 4
        identr_made, cross_made = sem("identr_made"), sem("cross_made")

        xg = x.rearrange("(g t p) d -> g p t d", p=P, t=GT)
        og = out.rearrange("(g t p) d -> g p t d", p=P, t=GT)
        ag = adj.rearrange("(g t q) j i -> g q j t i", q=2, t=GT)
        mats = [(w, l, m) for l in range(LAYERS) for m, w in enumerate((w_upper[l], w_lower[l], w_self[l]))]

        block = ctx.enter_context(nc.Block())

        @block.sync
        def _(sp):
            def weight(m):
                sp.dma_start(stage[m % 2][:, 0:KC, :], mats[m][0].rearrange("(k p) h -> p k h", p=P)).then_inc(w_in[m % 2], 16)

            def load(step, g, first=False):
                if not first:
                    sp.wait_ge(x_free[g], step)
                sp.dma_start(X[g][:, :, :], xg[step * PAIR + g]).then_inc(x_in[g], 16)
                if not first:
                    sp.wait_ge(a_free[g], step)
                for q in range(2):
                    sp.dma_start(A[g][q * NODES:(q + 1) * NODES, :, q * NODES:(q + 1) * NODES],
                                 ag[step * PAIR + g][q]).then_inc(a_in[g], 16)

            def store(step, g):
                sp.wait_ge(o_out, step * PAIR + g + 1)
                sp.dma_start(og[step * PAIR + g], O[g][:, :, :]).then_inc(stored[g], 16)

            weight(0)
            weight(1)
            for l in range(LAYERS):
                for dst, src in ((bias[:, l, UPPER], b_upper), (bias[:, l, LOWER], b_lower), (bias[:, l, SELF], b_self),
                                 (gain[:, l], ln_w), (beta[:, l], ln_b)):
                    sp.dma_start(dst, src[l].partition_broadcast(P)).then_inc(c_in, 16)
            sp.wait_ge(made, MADE)
            load(0, 0, first=True)
            for m in range(2, len(mats)):
                sp.wait_ge(w_lo, m - 1)
                weight(m)
            sp.wait_ge(w_lo, len(mats))
            load(0, 1, first=True)
            with sp.Fori(0, STEPS - 1, 1) as it:
                for g in range(PAIR):
                    load(it + 1, g)
                    store(it, g)
            for g in range(PAIR):
                store(STEPS - 1, g)
            for g in range(PAIR):
                sp.wait_ge(stored[g], (STEPS + 1) * 16)

        @block.tensor
        def _(pe):
            pe.wait_ge(made, MADE)
            for m, (_, l, kind) in enumerate(mats):
                pe.wait_ge(w_in[m % 2], 16 * (m // 2 + 1))
                if m >= 2:
                    pe.wait_ge(w_lo, m - 1)
                for c in range(KC):
                    for k in range(KC):
                        last = pe.transpose(bank[m % 2 * KC + c][:, k * P:(k + 1) * P], stage[m % 2][:, k, c * P:(c + 1) * P], ident[:, :])
                last.then_inc(w_t, 1)
            pe.wait_ge(w_lo, len(mats))
            pe.wait_ge(identr_made, 1)
            pe.wait_ge(cross_made, 2)
            pe.wait_ge(bank_full, jobs.ahead)

            def start(name, it):
                pe.wait_ge(drained, jobs.free(name, it))
                return bank[jobs.bank_of[name]]

            def head(it, l, g):
                if l == 0:
                    pe.wait_ge(a_in[g], (it + 1) * 32)
                    ps = start(("A", l, g, 0), it - (g == 0))
                    for t in range(GT):
                        last = pe.transpose(ps[:, t * P:(t + 1) * P], A[g][:, t, :], ident[:, :])
                    last.then_inc(bank_full, 1)
                    pe.wait_ge(x_in[g], (it + 1) * 16)
                else:
                    pe.wait_ge(o_ready, it * PAIR + g + 1)
                src = X[g] if l == 0 else O[g]
                for c in range(KC):
                    ps = start(("T", l, g, c), it - (l == 0 and g == 0))
                    for t in range(GT):
                        last = pe.transpose(ps[:, t * P:(t + 1) * P], src[:, t, c * P:(c + 1) * P], ident[:, :])
                    before_loop = isinstance(it, int) and it == 0 and l == 0 and g == 0 and c == KC - 1
                    last.then_inc(bank_full, 1 + jobs.behind if before_loop else 1)

            def scores(it, l, g):
                n = it * INST + (l * PAIR + g)
                pe.wait_ge(z_read, n + 1)
                pe.matmul(ubank[g][:, :], lhsT=identr[:, :], rhs=flat(cross[:, :, :]), start=True, stop=True)
                for c in range(KC):
                    pe.wait_ge(drained, jobs.drained(("T", l, g, c), it - (l == 0 and g == 0)))
                    for t in range(GT):
                        cols = slice(t * P, (t + 1) * P)
                        for j, (a, b) in enumerate(TERMS):
                            last = pe.matmul(ubank[g][:, cols], lhsT=HT[g][a][:, c, cols], rhs=HT[g][b][:, c, cols],
                                             start=False, stop=(c == KC - 1 and j == 2), skip_group_check=True)
                last.then_inc(u_full, 1)

            def shift(it, l, g):
                n = it * INST + (l * PAIR + g)
                pe.wait_ge(shift_ready, n + 1)
                pe.matmul(ubank[g][:, :], lhsT=ones[:, :], rhs=flat(SH[:, :, :]), start=False, stop=True,
                          skip_group_check=True).then_inc(u_shifted, 1)

            def row_sums(it, l, g):
                pe.wait_ge(e_done, it * INST + (l * PAIR + g + 1))
                for t in range(GT):
                    last = pe.matmul(ubank[g][:, 2 * t:2 * t + 2], lhsT=E[:, t, :], rhs=ones2[:, :], start=True, stop=True)
                last.then_inc(z_full, 1)

            def project(it, l, g, t):
                for m in (UPPER, LOWER, SELF):
                    ps = start(("R", l, g, (t, m)), it)
                    for c in range(KC):
                        for j, (a, b) in enumerate(TERMS):
                            last = pe.matmul(ps[:, 0:D], lhsT=HT[g][a][:, c, t * P:(t + 1) * P],
                                             rhs=W[l][m][b][:, c, :], start=(c == 0 and j == 0), stop=(c == KC - 1 and j == 2))
                    last.then_inc(bank_full, 1)

            def combine(it, l, g, tiles):
                n = it * INST + (l * PAIR + g)
                pe.wait_ge(p_lo, n + 2)
                for t in tiles:
                    ps = start(("C", l, g, t), it)
                    pe.wait_ge(hl_lo, n * (2 * GT) + (2 * t + 2 + SLOTS))
                    for side in (UPPER, LOWER):
                        for j, (a, b) in enumerate(TERMS):
                            last = pe.matmul(ps[:, 0:HLW], lhsT=PR[a][:, side, t, :], rhs=HL[b][:, side, t, :],
                                             start=(side == UPPER and j == 0), stop=(side == LOWER and j == 2))
                    last.then_inc(bank_full, 1)

            def body(it, last=False):
                for k in range(INST):
                    l, g = divmod(k, PAIR)
                    ahead = (it + (k == INST - 1), *following(k))
                    on = not (last and k == INST - 1)
                    project(it, l, g, 0)
                    row_sums(it, l, g)
                    project(it, l, g, 1)
                    project(it, l, g, 2)
                    if on:
                        head(*ahead)
                    project(it, l, g, 3)
                    if on:
                        scores(*ahead)
                    combine(it, l, g, range(0, GT // 2))
                    if on:
                        shift(*ahead)
                    combine(it, l, g, range(GT // 2, GT))

            for stage_of in (head, scores, shift):
                stage_of(0, 0, 0)
            with pe.Fori(0, STEPS - 1, 1) as it:
                body(it)
            body(STEPS - 1, last=True)

        @block.scalar
        def _(act):
            act.wait_ge(made, MADE)
            act.activation(identr[:, :], ident[:, :], ACT.Copy).then_inc(identr_made, 1)
            for m, (_, l, kind) in enumerate(mats):
                act.wait_ge(w_t, m + 1)
                for c in range(KC):
                    last = act.activation(W[l][kind][0][:, c, :], bank[m % 2 * KC + c][:, 0:D], ACT.Copy)
                last.then_inc(w_hi, 1)

            def split_t(it, l, g):
                for c in range(KC):
                    name, step = ("T", l, g, c), it - (l == 0 and g == 0)
                    act.wait_ge(bank_full, jobs.done(name, step))
                    act.activation(HT[g][0][:, c, :], bank[jobs.bank_of[name]][:, :], ACT.Relu if l else ACT.Copy).then_inc(ht_hi, 1)

            def exps(it, l, g):
                n = it * INST + (l * PAIR + g)
                act.wait_ge(es_done, n + 1)
                act.wait_ge(u_shifted, n + 1)
                act.activation(flat(E[:, :, :]), ubank[g][:, :], ACT.Exp, scale=TEMPER).then_inc(e_done, 1)

            def split_r(it, l, g, t):
                for m in (UPPER, LOWER):
                    act.wait_ge(drained, jobs.drained(("R", l, g, (t, m)), it))
                    act.activation(HL[0][:, m, t, 0:D], HB[:, (2 * t + m) % SLOTS, :], ACT.Copy).then_inc(hl_hi, 1)

            def split_p(it, l, g):
                pl, pg = divmod((l * PAIR + g - 1) % INST, PAIR)
                act.wait_ge(em_done, it * INST + (l * PAIR + g + 2))
                act.wait_ge(bank_full, jobs.done(("C", pl, pg, GT - 1), it - (l == 0 and g == 0)))
                act.activation(PR[0][:, :, :, :], EM[:, :, :, :], ACT.Copy).then_inc(p_hi, 1)

            def normalise(it, g):
                act.wait_ge(nb_ready, it * PAIR + (g + 1))
                for t in range(GT):
                    ins = act.activation(O[g][:, t, :], O[g][:, t, :], ACT.Identity, bias=NB[g][:, t:t + 1], scale=RS[g][:, t:t + 1])
                ins.then_inc(o_out, 1)

            def body(it, first=False, last=False):
                for k in range(INST):
                    l, g = divmod(k, PAIR)
                    ahead = (it + (k == INST - 1), *following(k))
                    on = not (last and k == INST - 1)
                    split_r(it, l, g, 0)
                    split_r(it, l, g, 1)
                    split_p(it, l, g)
                    split_r(it, l, g, 2)
                    if on:
                        split_t(*ahead)
                    split_r(it, l, g, 3)
                    if k == 0 and not first:
                        normalise(it - 1, 1)
                    if k == INST - 1:
                        normalise(it, 0)
                    if on:
                        exps(*ahead)

            split_t(0, 0, 0)
            exps(0, 0, 0)
            body(0, first=True)
            with act.Fori(1, STEPS - 1, 1) as it:
                body(it)
            body(STEPS - 1, last=True)
            normalise(STEPS - 1, 1)

        @block.gpsimd
        def _(pool):
            identity(pool, ident, zeroed, made)
            for g in range(PAIR):
                pool.memset(A[g][:, :, :], 0.0).then_inc(made, 1)
            pool.memset(as_f32(ones[:, :]), 1.0)
            pool.memset(ones2[:, :], 1.0).then_inc(p_lo, 1)
            pool.memset(scratch2[:, :, :], 0.0).then_inc(es_done, 1)
            pool.memset(mhalf[:, :], -0.5).then_inc(made, 1)
            pool.wait_ge(made, MADE)
            pool.memset(as_f32(HL[1][:, :, :, D:HLW]), 0.0)
            pool.memset(as_f32(HL[0][:, :, :, D:HLW]), 1.0).then_inc(hl_lo, SLOTS)

            def carry_wait(k):
                pool.tensor_tensor(scratch2[:, k, :], mhalf[:, :], mhalf[:, :], ALU.mult)

            def masks(it, g):
                if not (isinstance(it, int) and it == 0 and g == 0):
                    pool.wait_ge(em_done, it * INST + (PAIR + g + 2 - INST))
                pool.wait_ge(drained, jobs.drained(("A", 0, g, 0), it - (g == 0)))
                carry_wait(g)
                for m, (op, sign) in enumerate(((ALU.is_gt, 1), (ALU.is_gt, -1), (ALU.is_equal, 1))):
                    ins = pool.affine_select(out=AM[g][:, m], in_=AT[:, :, :], compare_op=op, fill=0.0, base=0,
                                             pattern=[[0, GT], [-sign, P]], channel_multiplier=sign)
                ins.then_inc(a_free[g], 1)

            def split_r(it, l, g, t):
                n = it * INST + (l * PAIR + g)
                for m in (UPPER, LOWER):
                    pool.wait_ge(hl_hi, n * (2 * GT) + (2 * t + m + 1))
                    pool.tensor_tensor(HL[1][:, m, t, 0:D], HB[:, (2 * t + m) % SLOTS, :], as_f32(HL[0][:, m, t, 0:D]),
                                       ALU.subtract).then_inc(hl_lo, 1)

            def diagonal(it, l, g):
                n = it * INST + (l * PAIR + g)
                if l == 0:
                    pool.wait_ge(a_free[g], it + 1)
                pool.wait_ge(dg_done, n + 1)
                pool.wait_ge(e_done, n + 1)
                pool.tensor_tensor(ES[:, :, :], E[:, :, :], AM[g][:, 2], ALU.mult).then_inc(es_done, 1)

            def split_p(it, l, g):
                pool.wait_ge(p_hi, it * INST + (l * PAIR + g + 1))
                pool.tensor_tensor(PR[1][:, :, :, :].rearrange("p s t i -> p (s t i)"), EM[:, :, :, :].rearrange("p s t i -> p (s t i)"),
                                   as_f32(PR[0][:, :, :, :]).rearrange("p s t i -> p (s t i)"), ALU.subtract).then_inc(p_lo, 1)

            def deviation(it, l, g):
                pool.wait_ge(var_ready, it * INST + (l * PAIR + g + 1))
                pool.tensor_tensor(FC[:, :], VV[:, :], mhalf[:, :], ALU.pow).then_inc(sd_ready, 1)

            def final_deviation(it, g):
                pool.wait_ge(var2_ready, it * PAIR + (g + 1))
                pool.tensor_tensor(RS[g][:, :], VE[:, :], mhalf[:, :], ALU.pow).then_inc(rs_ready, 1)

            def body(it, first=False, last=False):
                for k in range(INST):
                    l, g = divmod(k, PAIR)
                    on = not (last and k == INST - 1)
                    diagonal(it, l, g)
                    split_r(it, l, g, 0)
                    split_r(it, l, g, 1)
                    split_p(it, l, g)
                    split_r(it, l, g, 2)
                    if k == 0 and not first:
                        final_deviation(it - 1, 1)
                    if k == INST - 1:
                        final_deviation(it, 0)
                    split_r(it, l, g, 3)
                    if on and following(k)[0] == 0:
                        masks(it + (k == INST - 1), following(k)[1])
                    deviation(it, l, g)

            masks(0, 0)
            body(0, first=True)
            with pool.Fori(1, STEPS - 1, 1) as it:
                body(it)
            body(STEPS - 1, last=True)
            final_deviation(STEPS - 1, 1)

        V_RESIDUAL = 4 * GT - 1
        V_STEPS = INST * (3 * GT + 2) + PAIR * V_RESIDUAL

        @block.vector
        def _(dve):
            dve.memset(as_f32(cross[:, :, :]), 0.0).then_inc(cross_made, 1)
            dve.wait_ge(cross_made, 1)
            dve.memset(as_f32(cross[0:NODES, :, NODES:P]), CROSS)
            dve.memset(as_f32(cross[NODES:P, :, 0:NODES]), CROSS).then_inc(cross_made, 1)
            for m, (_, l, kind) in enumerate(mats):
                dve.wait_ge(w_hi, m + 1)
                for c in range(KC):
                    last = dve.tensor_tensor(W[l][kind][1][:, c, :], bank[m % 2 * KC + c][:, 0:D], as_f32(W[l][kind][0][:, c, :]), ALU.subtract)
                last.then_inc(w_lo, 1)
            dve.wait_ge(c_in, 16 * 5 * LAYERS)
            dve.wait_ge(made, MADE)
            dve.memset(scratch[:, 0:1], 0.0).then_inc(drained, CREDIT + jobs.ahead)
            dve.memset(scratch[:, 1:2], 0.0).then_inc(z_read, PAIR)
            for g in range(PAIR):
                dve.memset(scratch[:, 2 + g:3 + g], 0.0).then_inc(stored[g], 16)
            dve.memset(scratch[:, 4:5], 0.0).then_inc(dg_done, 1)
            dve.memset(scratch[:, 5:6], 0.0).then_inc(em_done, 1)

            dve.memset(scratch[:, 8:9], 0.0).then_inc(v_done, V_RESIDUAL)
            dve.memset(scratch[:, 9:10], 0.0).then_inc(bank_full, jobs.ahead)
            count = [0]

            def step(ins):
                count[0] += 1
                ins.then_inc(v_done, 1)
                return count[0]

            def own(it, k):
                dve.wait_ge(v_done, it * V_STEPS + k)

            def full(name, it):
                dve.wait_ge(bank_full, jobs.done(name, it))
                return bank[jobs.bank_of[name]]

            def masks(it, g):
                if not (isinstance(it, int) and it == 0 and g == 0):
                    dve.wait_ge(a_free[1 - g], it + g)
                dve.tensor_copy(flat(AT[:, :, :]), full(("A", 0, g, 0), it - (g == 0))[:, :]).then_inc(drained, 1)

            def split_t(it, l, g):
                for c in range(KC):
                    ps = full(("T", l, g, c), it - (l == 0 and g == 0))
                    dve.wait_ge(ht_hi, (it * INST + (l * PAIR + g)) * KC + (c + 1))
                    hi, lo = as_f32(HT[g][0][:, c, :]), HT[g][1][:, c, :]
                    before_loop = isinstance(it, int) and it == 0 and l == 0 and g == 0 and c == KC - 1
                    if l == 0:
                        dve.tensor_tensor(lo, ps[:, :], hi, ALU.subtract).then_inc(drained, 1 + jobs.behind if before_loop else 1)
                    else:
                        dve.scalar_tensor_tensor(lo, ps[:, :], 0.0, hi, ALU.max, ALU.subtract).then_inc(drained, 1)

            def maxima(it, l, g):
                n = it * INST + (l * PAIR + g)
                dve.wait_ge(u_full, n + 1)
                dve.tensor_reduce(MX[:, :], ubank[g][:, :].rearrange("p (t i) -> p t i", t=GT), AX.X, ALU.max).then_inc(mx_done, 1)
                dve.wait_ge(mx_done, n + 1)
                for t in range(GT):
                    ins = dve.tensor_scalar(SH[:, t, :], ident[:, :], MX[:, t:t + 1], -1.0, ALU.mult, ALU.mult)
                ins.then_inc(shift_ready, 1)

            def add_bias(it, l, g, t):
                n = it * INST + (l * PAIR + g)
                for m in (UPPER, LOWER, SELF):
                    ps = full(("R", l, g, (t, m)), it)
                    if m == SELF:
                        dst = HS[:, t, :]
                    else:
                        dve.wait_ge(hl_lo, n * (2 * GT) + (2 * t + m + 1))
                        dst = HB[:, (2 * t + m) % SLOTS, :]
                    dve.tensor_tensor(dst, ps[:, 0:D], bias[:, l, m], ALU.add).then_inc(drained, 1)

            def mask_exp(it, l, g):
                n = it * INST + (l * PAIR + g)
                if l == 0:
                    dve.wait_ge(a_free[g], it + 1)
                dve.wait_ge(p_lo, n + 1)
                dve.wait_ge(e_done, n + 1)
                for side in (UPPER, LOWER):
                    ins = dve.tensor_tensor(EM[:, side], E[:, :, :], AM[g][:, side], ALU.mult)
                ins.then_inc(em_done, 1)

            def diagonal(it, l, g):
                dve.wait_ge(es_done, it * INST + (l * PAIR + g + 2))
                dve.tensor_reduce(DG[:, :], ES[:, :, :], AX.X, ALU.add).then_inc(dg_done, 1)

            def statistics(it, l, g):
                n = it * INST + (l * PAIR + g)
                dve.wait_ge(dg_done, n + 2)
                dve.wait_ge(drained, jobs.drained(("R", l, g, (GT - 1, SELF)), it))
                if l == 0:
                    dve.wait_ge(stored[g], it * 16 + 16)
                for t in range(GT):
                    ps = full(("C", l, g, t), it)
                    step(dve.tensor_scalar(SS[:, t:t + 1], ps[:, D:D + 1], DG[:, t:t + 1], None, ALU.add))
                    dve.scalar_tensor_tensor(O[g][:, t, :], HS[:, t, :], DG[:, t:t + 1], ps[:, 0:D],
                                             ALU.mult, ALU.add).then_inc(drained, 1)
                for t in range(GT):
                    dve.wait_ge(drained, jobs.drained(("C", l, g, t), it))
                    s = step(dve.bn_stats(ST[:, t, :], O[g][:, t, :]))
                own(it, s)
                dve.tensor_scalar(scratch[:, 6:7], DG[:, 0:1], 0.0, None, ALU.mult)
                for t in range(GT):
                    s = step(dve.bn_aggr(MV[:, t, :], ST[:, t, :]))
                dve.wait_ge(z_full, n + 1)
                dve.scalar_tensor_tensor(DEN[:, :], ubank[g][:, 0:2 * GT:2], 1e-10, SS[:, :], ALU.mult, ALU.add).then_inc(z_read, 1)
                dve.wait_ge(z_read, n + 1 + PAIR)
                own(it, step(dve.tensor_tensor(D2[:, :], DEN[:, :], DEN[:, :], ALU.mult)))
                dve.scalar_tensor_tensor(VV[:, :], D2[:, :], 1e-12, MV[:, :, 1], ALU.mult, ALU.add).then_inc(var_ready, 1)
                for t in range(GT):
                    ins = dve.scalar_tensor_tensor(O[g][:, t, :], O[g][:, t, :], MV[:, t, 0:1], gain[:, l, :],
                                                   ALU.subtract, ALU.mult)
                step(ins)

            def finish(now, it, l, g):
                own(now, count[0])
                dve.wait_ge(sd_ready, it * INST + (l * PAIR + g + 1))
                s = {}
                for t in range(GT):
                    ins = dve.scalar_tensor_tensor(O[g][:, t, :], O[g][:, t, :], FC[:, t:t + 1], beta[:, l, :], ALU.mult, ALU.add)
                    if l == LAYERS - 1:
                        s[t] = step(ins)
                if l < LAYERS - 1:
                    ins.then_inc(o_ready, 1)
                    return
                for t in range(GT):
                    own(now, s[t])
                    ins = dve.scalar_tensor_tensor(O[g][:, t, :], O[g][:, t, :], 0.0, X[g][:, t, :], ALU.max, ALU.add)
                    if t == GT - 1:
                        ins.then_inc(x_free[g], 1)
                    else:
                        s[t] = step(ins)
                return s

            def final_statistics(now, it, g, s):
                for t in range(GT):
                    if t == GT - 1:
                        dve.wait_ge(x_free[g], it + 1)
                    else:
                        own(now, s[t])
                    s[t] = step(dve.bn_stats(ST2[:, t, :], O[g][:, t, :]))
                own(now, s[GT - 1])
                dve.tensor_scalar(scratch[:, 10 + g:11 + g], FC[:, 0:1], 0.0, None, ALU.mult)
                for t in range(GT):
                    s[t] = step(dve.bn_aggr(MV2[:, t, :], ST2[:, t, :]))
                own(now, s[GT - 1])
                dve.tensor_scalar(VE[:, :], MV2[:, :, 1], 1e-5, None, ALU.add).then_inc(var2_ready, 1)

            def minus_mean(it, g):
                dve.wait_ge(rs_ready, it * PAIR + (g + 1))
                dve.scalar_tensor_tensor(NB[g][:, :], MV2[:, :, 0], -1.0, RS[g][:, :], ALU.mult, ALU.mult).then_inc(nb_ready, 1)

            def body(it, first=False, last=False):
                count[0] = V_RESIDUAL if first else 0
                for k in range(INST):
                    l, g = divmod(k, PAIR)
                    ahead = (it + (k == INST - 1), *following(k))
                    on = not (last and k == INST - 1)
                    add_bias(it, l, g, 0)
                    before, ended = it if k else it - 1, None
                    if k or not first:
                        ended = finish(it, before, *divmod((k - 1) % INST, PAIR))
                    add_bias(it, l, g, 1)
                    mask_exp(it, l, g)
                    add_bias(it, l, g, 2)
                    if ended:
                        final_statistics(it, before, 1 - g, ended)
                    diagonal(it, l, g)
                    if on:
                        if ahead[1] == 0:
                            masks(ahead[0], ahead[2])
                        split_t(*ahead)
                    if ended:
                        minus_mean(before, 1 - g)
                    add_bias(it, l, g, 3)
                    if on:
                        maxima(*ahead)
                    statistics(it, l, g)
                assert count[0] == V_STEPS, (count[0], V_STEPS)

            masks(0, 0)
            split_t(0, 0, 0)
            maxima(0, 0, 0)
            body(0, first=True)
            with dve.Fori(1, STEPS - 1, 1) as it:
                body(it)
            body(STEPS - 1, last=True)
            count[0] = 0
            ended = finish(STEPS, STEPS - 1, LAYERS - 1, 1)
            final_statistics(STEPS, STEPS - 1, 1, ended)
            minus_mean(STEPS - 1, 1)


NAMES = ["x", "adj", "L0_gnn_W_left", "L0_gnn_W_right", "L0_gnn_W_lin", "L0_gnn_b_lin", "L0_gnn_ln_a", "L0_gnn_ln_b",
         "L1_gnn_Wl", "L1_gnn_bl", "L1_gnn_Ws", "L1_gnn_bs", "L1_gnn_Wr", "L1_gnn_br", "L1_gnn_ln_w", "L1_gnn_ln_b"]


def program(nc, a, x1, out):
    network0(nc, a["x"], a["adj"], a["L0_gnn_W_left"], a["L0_gnn_W_right"], a["L0_gnn_W_lin"],
             a["L0_gnn_b_lin"], a["L0_gnn_ln_a"], a["L0_gnn_ln_b"], x1)
    network1(nc, x1, a["adj"], a["L1_gnn_Wl"], a["L1_gnn_bl"], a["L1_gnn_Ws"], a["L1_gnn_bs"],
             a["L1_gnn_Wr"], a["L1_gnn_br"], a["L1_gnn_ln_w"], a["L1_gnn_ln_b"], out)


def kernel(**inputs):
    import concourse.bacc as bacc
    from concourse.bass_utils import run_bass_kernel_spmd as run
    nc = bacc.Bacc("TRN2", target_bir_lowering=False, num_devices=1)
    arrays, aps = {}, {}
    for name in NAMES:
        v = np.ascontiguousarray(inputs[name])
        if name == "x":
            v = v.reshape(GRAPHS * NODES, D)
        arrays["in_" + name] = v
        aps[name] = nc.dram_tensor("in_" + name, v.shape, F32, kind="ExternalInput").ap()
    x1 = nc.dram_tensor("x1", (GRAPHS * NODES, D), F32, kind="Internal").ap()
    out = nc.dram_tensor("out", (GRAPHS * NODES, D), F32, kind="ExternalOutput").ap()
    program(nc, aps, x1, out)
    r = run(nc, [arrays], core_ids=[0])
    return r.results[0]["out"].reshape(GRAPHS, NODES, D)
```

```python
import numpy as np
import concourse.bass as bass
from concourse import mybir
from contextlib import ExitStack

F32 = mybir.dt.float32
F32R = mybir.dt.float32r
ALU = mybir.AluOpType
ACT = mybir.ActivationFunctionType
AX = mybir.AxisListType

GRAPHS, NODES, D = 128, 64, 384
LAYERS = 2
P = 128
KC = D // P
GT = 4
GROUPS = GRAPHS * NODES // (GT * P)
PAIR = 2
STEPS = GROUPS // PAIR
INST = LAYERS * PAIR
RING = 6
CREDIT = RING
HLW = D + 2
TEMPER = 1.0 / float(np.sqrt(D))
CROSS = -float(2.0 ** 100)
TERMS = ((0, 0), (0, 1), (1, 0))


class Plan:

    def __init__(self, body, last, head, skip_at=0):
        self.jobs, self.body, self.last = len(body), body, last
        self.ahead = body.index(head[0])
        self.behind = len(body) - self.ahead - len(head)
        assert body[self.ahead:self.ahead + len(head)] == head
        skip = -len(body) % RING
        self.bank_of = {name: (p + (skip if p >= skip_at else 0)) % RING for p, name in enumerate(body)}
        for before, name in zip(last, last[1:]):
            self.bank_of.setdefault(name, (self.bank_of[before] + 1) % RING)
        self.need = {}
        for which, steps in (("body", (body, body)), ("last", (body, last))):
            user, n = {}, 0
            for step in steps:
                for name in step:
                    self.need[which, name] = user.get(self.bank_of[name], -len(body)) - len(body) + 1 + CREDIT
                    user[self.bank_of[name]] = n
                    n += 1

    def done(self, name, step):
        order = self.last if isinstance(step, int) and step == STEPS - 1 else self.body
        return (step + 1) * self.jobs + (order.index(name) + 1)

    def drained(self, name, step):
        return self.done(name, step) + CREDIT

    def free(self, name, step):
        which = "last" if isinstance(step, int) and step == STEPS - 1 else "body"
        return (step + 1) * self.jobs + self.need[which, name]


def following(k):
    return divmod((k + 1) % INST, PAIR)


def as_f32(ap):
    return ap.bitcast(F32)


def flat(ap):
    return ap.rearrange("p t i -> p (t i)")


def identity(pool, ident, zeroed, made):
    pool.memset(ident[:, :], 0.0).then_inc(zeroed, 1)
    pool.wait_ge(zeroed, 1)
    pool.affine_select(out=ident[:, :], in_=ident[:, :], compare_op=ALU.not_equal, fill=1.0, base=0,
                       pattern=[[-1, P]], channel_multiplier=1).then_inc(made, 1)




class Core:

    def __init__(self, nc, ctx, next_weights):
        def sb(name, shape, dt=F32):
            return ctx.enter_context(nc.sbuf_tensor("core_" + name, shape, dt))

        def sem(name):
            return ctx.enter_context(nc.semaphore("core_" + name))

        self.ident = sb("ident", [P, P])
        self.W = [[[sb(f"w{l}{m}{s}", [P, KC, D], F32R) for s in range(2)] for m in range(3)] for l in range(LAYERS)]
        self.X = [sb(f"x{g}", [P, GT, D]) for g in range(PAIR)]
        self.O = [sb(f"o{g}", [P, GT, D]) for g in range(PAIR)]
        self.A = [sb(f"a{g}", [P, GT, P]) for g in range(PAIR)]
        self.bank = [ctx.enter_context(nc.psum_tensor(f"core_bank{i}", [P, 512], F32)) for i in range(RING)]
        self.ubank = [ctx.enter_context(nc.psum_tensor(f"core_u{i}", [P, 512], F32)) for i in range(PAIR)]
        self.next_mats = [(next_weights[m][l], l, m) for l in range(LAYERS) for m in range(3)]
        self.next_w_in = [sem(f"next_w_in{m}") for m in range(len(self.next_mats))]
        self.next_w_hi = sem("next_w_hi")
        self.next_x_in, self.next_a_in = sem("next_x_in"), sem("next_a_in")
        self.stored = [sem(f"stored{g}") for g in range(PAIR)]
        self.all_stored = (STEPS + 1) * 16
def network0(nc, core, x, adj, w_left, w_right, w_lin, b_lin, ln_a, ln_b, out):
    EARLY, LATE = range(0, 2), range(2, len(core.next_mats))

    def plan(last):
        order = []
        for k in range(INST):
            l, g = divmod(k, PAIR)
            pl, pg = divmod(k - 1, PAIR)
            nl, ng = following(k)
            head = [("A", nl, ng, 0)] if nl == 0 else []
            head += [("T", nl, ng, c) for c in range(KC)]
            order += [("N", l, g, i) for i in range(KC)]
            order += [("C", pl, pg, t) for t in range(GT)] if k else []
            order += [("N", l, g, i) for i in range(KC, 2 * KC)]
            order += [("H", l, g, t) for t in range(GT - 1)]
            if k < INST - 1:
                order += head + [("H", l, g, GT - 1)]
            else:
                order += [("H", l, g, GT - 1)] + ([] if last else head)
                order += [("W", i, c) for i in EARLY for c in range(KC)] if last else []
                order += [("C", l, g, t) for t in range(GT)]
                order += [("W", i, c) for i in LATE for c in range(KC)] if last else []
        return order

    HEAD = [("A", 0, 0, 0)] + [("T", 0, 0, c) for c in range(KC)]
    jobs = Plan(plan(False), plan(True), HEAD, skip_at=plan(False).index(("H", 0, 1, 0)))
    SLOTS = 4

    ctx = ExitStack()
    with ctx:
        def sb(name, shape, dt=F32):
            return ctx.enter_context(nc.sbuf_tensor("n0_" + name, shape, dt))

        def sem(name):
            return ctx.enter_context(nc.semaphore("n0_" + name))

        ident, W, X, O, A, bank, ubank = core.ident, core.W, core.X, core.O, core.A, core.bank, core.ubank
        bias, gain, beta = (sb(n, [P, LAYERS, D]) for n in ("bias", "gain", "beta"))
        AT = [sb(f"at{g}", [P, GT, P]) for g in range(PAIR)]
        SM = [sb(f"sm{g}", [P, GT, 2, P]) for g in range(PAIR)]
        HT = [[sb(f"ht{g}{s}", [P, KC, GT * P], F32R) for s in range(2)] for g in range(PAIR)]
        N = [sb(f"n{s}", [P, KC, 2, GT * P], F32R) for s in range(2)]
        HB = sb("hb", [P, SLOTS, D])
        HL = [sb(f"hl{s}", [P, GT, HLW], F32R) for s in range(2)]
        UM = [sb(f"um{k}", [P, 2, 2, P]) for k in range(2)]
        E = sb("e", [P, GT, P])
        PR = [sb(f"p{s}", [P, GT, P], F32R) for s in range(2)]
        half, mhalf = sb("half", [P, GT]), sb("mhalf", [P, GT])
        ST, MV = sb("st", [P, GT, 6]), sb("mv", [P, GT, 2])
        WS, SD, FC = sb("ws", [P, GT]), sb("sd", [P, GT]), sb("fc", [P, GT])
        ST2, MV2, VE = sb("st2", [P, GT, 6]), sb("mv2", [P, GT, 2]), sb("ve", [P, GT])
        RS, NB = ([sb(f"{n}{g}", [P, GT]) for g in range(PAIR)] for n in ("rs", "nb"))
        scratch, scratch2 = sb("scratch", [P, 8]), sb("scratch2", [P, 4, GT])

        raw = [sb(f"raw{i}", [P, KC, D]) for i in range(4)]
        stage = [r[:, :, :] for r in raw] + [o[:, 0:KC, :] for o in O]

        bank_full = sem("bank_full")
        drained = sem("drained")
        x_in, a_in, x_free, a_free = ([sem(f"{n}{g}") for g in range(PAIR)] for n in ("x_in", "a_in", "x_free", "a_free"))
        stored = core.stored
        ht_hi, n_hi = sem("ht_hi"), sem("n_hi")
        u_full, u_masked, u_added = sem("u_full"), sem("u_masked"), sem("u_added")
        e_done, p_done, p_hi, p_lo = sem("e_done"), sem("p_done"), sem("p_hi"), sem("p_lo")
        hl_hi, hl_lo = sem("hl_hi"), sem("hl_lo")
        var_ready, sd_ready, o_ready, var2_ready, rs_ready, nb_ready, o_out = (
            sem(n) for n in ("var_ready", "sd_ready", "o_ready", "var2_ready", "rs_ready", "nb_ready", "o_out"))
        v_done = sem("v_done")
        w_in = [sem(f"w_in{m}") for m in range(len(stage))]
        c_in, w_hi, w_lo, w_t, zeroed, made = (sem(n) for n in ("c_in", "w_hi", "w_lo", "w_t", "zeroed", "made"))
        MADE = 4

        xg = x.rearrange("(g t p) d -> g p t d", p=P, t=GT)
        og = out.rearrange("(g t p) d -> g p t d", p=P, t=GT)
        ag = adj.rearrange("(g t q) j i -> g q j t i", q=2, t=GT)
        LEFT, RIGHT, LIN = range(3)
        mats = [(w_left[0], 0, LEFT), (w_right[0], 0, RIGHT), (w_lin[0], 0, LIN),
                (w_lin[1], 1, LIN), (w_left[1], 1, LEFT), (w_right[1], 1, RIGHT)]
        HEAD_MATS = 4

        block = ctx.enter_context(nc.Block())

        @block.sync
        def _(sp):
            def weight(m):
                sp.dma_start(stage[m], mats[m][0].rearrange("(k p) h -> p k h", p=P)).then_inc(w_in[m], 16)

            def next_weight(i):
                sp.dma_start(raw[i % len(raw)][:, :, :], core.next_mats[i][0].rearrange("(k p) h -> p k h", p=P)).then_inc(core.next_w_in[i], 16)

            def load(step, g, first=False):
                if not first:
                    sp.wait_ge(a_free[g], step)
                for q in range(2):
                    sp.dma_start(A[g][q * NODES:(q + 1) * NODES, :, q * NODES:(q + 1) * NODES],
                                 ag[step * PAIR + g][q]).then_inc(a_in[g], 16)
                if not first:
                    sp.wait_ge(x_free[g], step)
                sp.dma_start(X[g][:, :, :], xg[step * PAIR + g]).then_inc(x_in[g], 16)

            def store(step, g):
                sp.wait_ge(o_out, step * PAIR + g + 1)
                sp.dma_start(og[step * PAIR + g], O[g][:, :, :]).then_inc(stored[g], 16)

            for m in range(HEAD_MATS):
                weight(m)
            sp.wait_ge(made, MADE)
            load(0, 0, first=True)
            for m in range(HEAD_MATS, len(mats)):
                weight(m)
            for l in range(LAYERS):
                for dst, src in ((bias, b_lin), (gain, ln_a), (beta, ln_b)):
                    sp.dma_start(dst[:, l], src[l].partition_broadcast(P)).then_inc(c_in, 16)
            load(0, 1, first=True)
            for i in range(len(raw)):
                sp.wait_ge(w_lo, i + 1)
                next_weight(i)
            with sp.Fori(0, STEPS - 1, 1) as it:
                for g in range(PAIR):
                    load(it + 1, g)
                    store(it, g)
            sp.wait_ge(x_free[0], STEPS)
            sp.wait_ge(a_free[0], STEPS)
            sp.wait_ge(stored[0], 2 * 16)
            sp.dma_start(X[0][:, :, :], og[0]).then_inc(core.next_x_in, 16)
            for q in range(2):
                sp.dma_start(A[0][q * NODES:(q + 1) * NODES, :, q * NODES:(q + 1) * NODES], ag[0][q]).then_inc(core.next_a_in, 16)
            for i in range(len(raw), len(core.next_mats)):
                sp.wait_ge(bank_full, jobs.done(("W", i - len(raw), KC - 1), STEPS - 1))
                next_weight(i)
            store(STEPS - 1, 0)
            store(STEPS - 1, 1)

        @block.tensor
        def _(pe):
            pe.wait_ge(made, MADE)
            for m, (_, l, kind) in enumerate(mats):
                if kind == LIN:
                    pe.wait_ge(w_in[m], 16)
                    for c in range(KC):
                        for k in range(KC):
                            last = pe.transpose(bank[l * KC + c][:, k * P:(k + 1) * P], stage[m][:, k, c * P:(c + 1) * P], ident[:, :])
                    last.then_inc(w_t, 1)
            pe.wait_ge(w_lo, HEAD_MATS)
            pe.wait_ge(bank_full, jobs.ahead)

            def start(name, it):
                pe.wait_ge(drained, jobs.free(name, it))
                return bank[jobs.bank_of[name]]

            def head(it, l, g):
                if l == 0:
                    pe.wait_ge(a_in[g], (it + 1) * 32)
                    ps = start(("A", l, g, 0), it - (g == 0))
                    for t in range(GT):
                        last = pe.transpose(ps[:, t * P:(t + 1) * P], A[g][:, t, :], ident[:, :])
                    last.then_inc(bank_full, 1)
                    pe.wait_ge(x_in[g], (it + 1) * 16)
                else:
                    pe.wait_ge(o_ready, it * PAIR + g + 1)
                src = X[g] if l == 0 else O[g]
                for c in range(KC):
                    ps = start(("T", l, g, c), it - (l == 0 and g == 0))
                    for t in range(GT):
                        last = pe.transpose(ps[:, t * P:(t + 1) * P], src[:, t, c * P:(c + 1) * P], ident[:, :])
                    before_loop = isinstance(it, int) and it == 0 and l == 0 and g == 0 and c == KC - 1
                    last.then_inc(bank_full, 1 + jobs.behind if before_loop else 1)

            def project_scores(it, l, g, i):
                side, c = i // KC, i % KC
                ps = start(("N", l, g, i), it)
                for k in range(KC):
                    if i == 0:
                        pe.wait_ge(drained, jobs.drained(("T", l, g, k), it - (l == 0 and g == 0)))
                    for j, (a, b) in enumerate(TERMS):
                        last = pe.matmul(ps[:, :], lhsT=W[l][side][a][:, k, c * P:(c + 1) * P],
                                         rhs=HT[g][b][:, k, :], start=(k == 0 and j == 0), stop=(k == KC - 1 and j == 2))
                last.then_inc(bank_full, 1)

            def scores(it, l, g):
                n = it * INST + (l * PAIR + g)
                pe.wait_ge(drained, jobs.drained(("N", l, g, 2 * KC - 1), it))
                for k in range(2):
                    pe.wait_ge(u_masked, n * 2 + (k + 1))
                    for t in range(2):
                        cols = slice((2 * k + t) * P, (2 * k + t + 1) * P)
                        for c in range(KC):
                            for j, (a, b) in enumerate(TERMS):
                                last = pe.matmul(ubank[k][:, t * 2 * P:(t + 1) * 2 * P], lhsT=HT[g][a][:, c, cols],
                                                 rhs=N[b][:, c, :, cols], start=(c == 0 and j == 0), stop=(c == KC - 1 and j == 2))
                    last.then_inc(u_full, 1)

            def project(it, l, g, t):
                ps = start(("H", l, g, t), it)
                for c in range(KC):
                    for j, (a, b) in enumerate(TERMS):
                        last = pe.matmul(ps[:, 0:D], lhsT=HT[g][a][:, c, t * P:(t + 1) * P],
                                         rhs=W[l][2][b][:, c, :], start=(c == 0 and j == 0), stop=(c == KC - 1 and j == 2))
                last.then_inc(bank_full, 1)

            def combine(it, l, g):
                n = it * INST + (l * PAIR + g)
                for t in range(GT):
                    ps = start(("C", l, g, t), it)
                    pe.wait_ge(p_lo, n * 2 + (t // 2 + 1 + 2))
                    pe.wait_ge(hl_lo, n * GT + (t + 1 + SLOTS))
                    for j, (a, b) in enumerate(TERMS):
                        last = pe.matmul(ps[:, 0:HLW], lhsT=PR[a][:, t, :], rhs=HL[b][:, t, :], start=(j == 0), stop=(j == 2))
                    last.then_inc(bank_full, 1)

            def next_weights(which):
                for i in which:
                    pe.wait_ge(core.next_w_in[i], 16)
                    for c in range(KC):
                        ps = start(("W", i, c), STEPS - 1)
                        for k in range(KC):
                            last = pe.transpose(ps[:, k * P:(k + 1) * P], raw[i % len(raw)][:, k, c * P:(c + 1) * P], ident[:, :])
                        last.then_inc(bank_full, 1)

            def body(it, last=False):
                for k in range(INST):
                    l, g = divmod(k, PAIR)
                    nl, ng = following(k)
                    for i in range(KC):
                        project_scores(it, l, g, i)
                    if k:
                        combine(it, *divmod(k - 1, PAIR))
                    for i in range(KC, 2 * KC):
                        project_scores(it, l, g, i)
                    project(it, l, g, 0)
                    scores(it, l, g)
                    project(it, l, g, 1)
                    project(it, l, g, 2)
                    if k < INST - 1:
                        head(it, nl, ng)
                        project(it, l, g, 3)
                    else:
                        project(it, l, g, 3)
                        if last:
                            next_weights(EARLY)
                        else:
                            head(it + 1, nl, ng)
                        combine(it, l, g)
                        if last:
                            next_weights(LATE)

            head(0, 0, 0)
            with pe.Fori(0, STEPS - 1, 1) as it:
                body(it)
            body(STEPS - 1, last=True)

        @block.scalar
        def _(act):
            def split_weight(m):
                _, l, kind = mats[m]
                if kind == LIN:
                    act.wait_ge(w_t, l + 1)
                    for c in range(KC):
                        last = act.activation(W[l][kind][0][:, c, :], bank[l * KC + c][:, 0:D], ACT.Copy)
                else:
                    act.wait_ge(w_in[m], 16)
                    last = act.activation(W[l][kind][0][:, :, :], stage[m], ACT.Copy)
                last.then_inc(w_hi, 1)

            def next_weight(i):
                _, l, m = core.next_mats[i]
                for c in range(KC):
                    act.wait_ge(bank_full, jobs.done(("W", i, c), STEPS - 1))
                    act.activation(W[l][m][0][:, c, :], bank[jobs.bank_of["W", i, c]][:, 0:D], ACT.Copy).then_inc(core.next_w_hi, 1)

            def split_t(it, l, g):
                for c in range(KC):
                    name, step = ("T", l, g, c), it - (l == 0 and g == 0)
                    act.wait_ge(bank_full, jobs.done(name, step))
                    act.activation(HT[g][0][:, c, :], bank[jobs.bank_of[name]][:, :], ACT.Relu if l else ACT.Copy).then_inc(ht_hi, 1)

            def split_n(it, l, g):
                for i in range(2 * KC):
                    name = ("N", l, g, i)
                    act.wait_ge(bank_full, jobs.done(name, it))
                    act.activation(N[0][:, i % KC, i // KC, :], bank[jobs.bank_of[name]][:, :], ACT.Copy).then_inc(n_hi, 1)

            def exps(it, l, g):
                n = it * INST + (l * PAIR + g)
                for k in range(2):
                    act.wait_ge(u_added, n * 2 + (k + 1 + 2))
                    act.activation(E[:, 2 * k:2 * k + 2, :], E[:, 2 * k:2 * k + 2, :], ACT.Exp, scale=TEMPER).then_inc(e_done, 1)

            def split_p(it, l, g):
                n = it * INST + (l * PAIR + g)
                for k in range(2):
                    act.wait_ge(p_done, n * 2 + (k + 1 + 2))
                    act.activation(PR[0][:, 2 * k:2 * k + 2, :], E[:, 2 * k:2 * k + 2, :], ACT.Copy).then_inc(p_hi, 1)

            def split_h(it, l, g, t):
                act.wait_ge(drained, jobs.drained(("H", l, g, t), it))
                act.activation(HL[0][:, t, 0:D], HB[:, t % SLOTS, :], ACT.Copy).then_inc(hl_hi, 1)

            def normalise(it, g):
                act.wait_ge(nb_ready, it * PAIR + (g + 1))
                for t in range(GT):
                    ins = act.activation(O[g][:, t, :], O[g][:, t, :], ACT.Identity, bias=NB[g][:, t:t + 1], scale=RS[g][:, t:t + 1])
                ins.then_inc(o_out, 1)

            def body(it, first=False, last=False):
                for k in range(INST):
                    l, g = divmod(k, PAIR)
                    nl, ng = following(k)
                    split_n(it, l, g)
                    split_h(it, l, g, 0)
                    exps(it, l, g)
                    split_h(it, l, g, 1)
                    split_h(it, l, g, 2)
                    if k < INST - 1:
                        split_t(it, nl, ng)
                        split_p(it, l, g)
                        split_h(it, l, g, 3)
                    else:
                        if last:
                            next_weight(EARLY[0])
                        split_p(it, l, g)
                        if not last:
                            split_t(it + 1, nl, ng)
                        split_h(it, l, g, 3)
                        if last:
                            next_weight(EARLY[1])
                    if k == 0 and not first:
                        normalise(it - 1, 1)
                    if k == INST - 1:
                        normalise(it, 0)

            for m in range(HEAD_MATS):
                split_weight(m)
            split_t(0, 0, 0)
            for m in range(HEAD_MATS, len(mats)):
                split_weight(m)
            body(0, first=True)
            with act.Fori(1, STEPS - 1, 1) as it:
                body(it)
            body(STEPS - 1, last=True)
            for i in LATE:
                next_weight(i)
            normalise(STEPS - 1, 1)

        @block.gpsimd
        def _(pool):
            identity(pool, ident, zeroed, made)
            for g in range(PAIR):
                pool.memset(A[g][:, :, :], 0.0).then_inc(made, 1)
            pool.memset(half[:, :], 0.5).then_inc(p_done, 2)
            pool.memset(scratch2[:, :, :], 0.0).then_inc(u_added, 2)
            pool.memset(mhalf[:, :], -0.5).then_inc(made, 1)
            pool.wait_ge(made, MADE)
            pool.memset(as_f32(HL[1][:, :, D:HLW]), 0.0).then_inc(p_lo, 2)
            pool.memset(as_f32(HL[0][:, :, D:HLW]), 1.0).then_inc(hl_lo, SLOTS)

            def carry_wait(k):
                pool.tensor_tensor(scratch2[:, k, :], half[:, :], half[:, :], ALU.mult)

            def masks(it, g):
                first = isinstance(it, int) and it == 0 and g == 0
                if not first:
                    pool.wait_ge(u_masked, it * (2 * INST) + (2 * (PAIR + g + 1 - INST) + 2))
                pool.wait_ge(drained, jobs.drained(("A", 0, g, 0), it - (g == 0)))
                carry_wait(g)
                pool.affine_select(out=SM[g][:, :, 1, :], in_=A[g][:, :, :], compare_op=ALU.is_gt, fill=0.0, base=0,
                                   pattern=[[0, GT], [1, P]], channel_multiplier=-1)
                pool.affine_select(out=SM[g][:, :, 0, :], in_=AT[g][:, :, :], compare_op=ALU.is_ge, fill=0.0, base=0,
                                   pattern=[[0, GT], [-1, P]], channel_multiplier=1).then_inc(a_free[g], 1)

            def add_scores(it, l, g):
                n = it * INST + (l * PAIR + g)
                pool.wait_ge(p_lo, n * 2 + 2)
                for k in range(2):
                    pool.wait_ge(u_masked, n * 2 + (k + 1 + 2))
                    pool.tensor_tensor(E[:, 2 * k:2 * k + 2, :], UM[k][:, :, 0, :], UM[k][:, :, 1, :], ALU.add).then_inc(u_added, 1)

            def mask_exp(it, l, g):
                n = it * INST + (l * PAIR + g)
                for k in range(2):
                    pool.wait_ge(e_done, n * 2 + (k + 1))
                    pool.tensor_tensor(E[:, 2 * k:2 * k + 2, :], E[:, 2 * k:2 * k + 2, :], AT[g][:, 2 * k:2 * k + 2, :],
                                       ALU.mult).then_inc(p_done, 1)

            def split_p(it, l, g):
                n = it * INST + (l * PAIR + g)
                for k in range(2):
                    pool.wait_ge(p_hi, n * 2 + (k + 1))
                    pool.tensor_tensor(PR[1][:, 2 * k:2 * k + 2, :], E[:, 2 * k:2 * k + 2, :],
                                       as_f32(PR[0][:, 2 * k:2 * k + 2, :]), ALU.subtract).then_inc(p_lo, 1)

            def split_h(it, l, g, t):
                pool.wait_ge(hl_hi, (it * INST + (l * PAIR + g)) * GT + (t + 1))
                pool.tensor_tensor(HL[1][:, t, 0:D], HB[:, t % SLOTS, :], as_f32(HL[0][:, t, 0:D]), ALU.subtract).then_inc(hl_lo, 1)

            def deviation(it, l, g):
                pool.wait_ge(var_ready, it * INST + (l * PAIR + g + 1))
                pool.tensor_tensor(SD[:, :], MV[:, :, 1], half[:, :], ALU.pow).then_inc(sd_ready, 1)

            def final_deviation(it, g):
                pool.wait_ge(var2_ready, it * PAIR + (g + 1))
                pool.tensor_tensor(RS[g][:, :], VE[:, :], mhalf[:, :], ALU.pow).then_inc(rs_ready, 1)

            def body(it, first=False, last=False):
                for k in range(INST):
                    l, g = divmod(k, PAIR)
                    nl, ng = following(k)
                    if k:
                        deviation(it, *divmod(k - 1, PAIR))
                    if k < INST - 1:
                        split_h(it, l, g, 0)
                    add_scores(it, l, g)
                    if k == INST - 1:
                        split_h(it, l, g, 0)
                    if k < INST - 1:
                        split_h(it, l, g, 1)
                    mask_exp(it, l, g)
                    if k == INST - 1:
                        split_h(it, l, g, 1)
                    else:
                        split_h(it, l, g, 2)
                    split_p(it, l, g)
                    if k == INST - 1:
                        split_h(it, l, g, 2)
                    if k == 0 and not first:
                        final_deviation(it - 1, 1)
                    if k == 0:
                        masks(it, 1)
                    split_h(it, l, g, 3)
                    if k == INST - 1:
                        final_deviation(it, 0)
                        if not last:
                            masks(it + 1, 0)
                        deviation(it, l, g)

            masks(0, 0)
            body(0, first=True)
            with pool.Fori(1, STEPS - 1, 1) as it:
                body(it)
            body(STEPS - 1, last=True)
            final_deviation(STEPS - 1, 1)

        V_FINISH, V_RESIDUAL = 2, 4 * GT - 1
        V_STEPS = INST * (3 * GT - 1 + V_FINISH) + PAIR * V_RESIDUAL

        @block.vector
        def _(dve):
            def split_weight(m):
                _, l, kind = mats[m]
                dve.wait_ge(w_hi, m + 1)
                if kind == LIN:
                    for c in range(KC):
                        last = dve.tensor_tensor(W[l][kind][1][:, c, :], bank[l * KC + c][:, 0:D], as_f32(W[l][kind][0][:, c, :]), ALU.subtract)
                else:
                    last = dve.tensor_tensor(W[l][kind][1][:, :, :], stage[m], as_f32(W[l][kind][0][:, :, :]), ALU.subtract)
                last.then_inc(w_lo, 1)

            def next_weight(i):
                _, l, m = core.next_mats[i]
                for c in range(KC):
                    dve.wait_ge(core.next_w_hi, i * KC + c + 1)
                    dve.tensor_tensor(W[l][m][1][:, c, :], bank[jobs.bank_of["W", i, c]][:, 0:D],
                                      as_f32(W[l][m][0][:, c, :]), ALU.subtract).then_inc(drained, 1)

            for m in range(HEAD_MATS):
                split_weight(m)
            dve.memset(scratch[:, 0:1], 0.0).then_inc(drained, CREDIT + jobs.ahead)
            dve.memset(scratch[:, 1:2], 0.0).then_inc(u_masked, 2)
            for g in range(PAIR):
                dve.memset(scratch[:, 2 + g:3 + g], 0.0).then_inc(stored[g], 16)

            dve.memset(scratch[:, 4:5], 0.0).then_inc(v_done, V_FINISH + V_RESIDUAL)
            dve.memset(scratch[:, 5:6], 0.0).then_inc(bank_full, jobs.ahead)
            count = [0]

            def step(ins):
                count[0] += 1
                ins.then_inc(v_done, 1)
                return count[0]

            def own(it, k):
                dve.wait_ge(v_done, it * V_STEPS + k)

            def full(name, it):
                dve.wait_ge(bank_full, jobs.done(name, it))
                return bank[jobs.bank_of[name]]

            def masks(it, g):
                first = isinstance(it, int) and it == 0 and g == 0
                if not first:
                    dve.wait_ge(p_done, it * (2 * INST) + (2 * (PAIR + g + 1 - INST) + 2))
                dve.tensor_copy(flat(AT[g][:, :, :]), full(("A", 0, g, 0), it - (g == 0))[:, :]).then_inc(drained, 1)

            def split_t(it, l, g):
                for c in range(KC):
                    ps = full(("T", l, g, c), it - (l == 0 and g == 0))
                    dve.wait_ge(ht_hi, (it * INST + (l * PAIR + g)) * KC + (c + 1))
                    hi, lo = as_f32(HT[g][0][:, c, :]), HT[g][1][:, c, :]
                    before_loop = isinstance(it, int) and it == 0 and l == 0 and g == 0 and c == KC - 1
                    if l == 0:
                        dve.tensor_tensor(lo, ps[:, :], hi, ALU.subtract).then_inc(drained, 1 + jobs.behind if before_loop else 1)
                    else:
                        dve.scalar_tensor_tensor(lo, ps[:, :], 0.0, hi, ALU.max, ALU.subtract).then_inc(drained, 1)

            def split_n(it, l, g, i):
                ps = full(("N", l, g, i), it)
                dve.wait_ge(n_hi, (it * INST + (l * PAIR + g)) * (2 * KC) + (i + 1))
                dve.tensor_tensor(N[1][:, i % KC, i // KC, :], ps[:, :], as_f32(N[0][:, i % KC, i // KC, :]),
                                  ALU.subtract).then_inc(drained, 1)

            def mask_scores(it, l, g):
                n = it * INST + (l * PAIR + g)
                dve.wait_ge(u_added, n * 2 + 2)
                if l == 0:
                    dve.wait_ge(a_free[g], it + 1)
                for k in range(2):
                    dve.wait_ge(u_full, n * 2 + (k + 1))
                    dve.tensor_tensor(UM[k][:, :, :, :].rearrange("p t s i -> p (t s i)"), ubank[k][:, :],
                                      SM[g][:, 2 * k:2 * k + 2, :, :].rearrange("p t s i -> p (t s i)"),
                                      ALU.mult).then_inc(u_masked, 1)

            def add_bias(it, l, g, t):
                ps = full(("H", l, g, t), it)
                dve.wait_ge(hl_lo, (it * INST + (l * PAIR + g)) * GT + (t + 1))
                dve.tensor_tensor(HB[:, t % SLOTS, :], ps[:, 0:D], bias[:, l, :], ALU.add).then_inc(drained, 1)

            def statistics(it, l, g):
                if l == 0:
                    dve.wait_ge(stored[g], it * 16 + 16)
                for t0 in range(0, GT, 2):
                    pair = (t0, t0 + 1)
                    ps = {t: bank[jobs.bank_of["C", l, g, t]] for t in pair}
                    a = {}
                    for t in pair:
                        s = step(dve.bn_stats(ST[:, t, :], full(("C", l, g, t), it)[:, 0:D]))
                    own(it, s)
                    for t in pair:
                        step(dve.tensor_scalar(WS[:, t:t + 1], ps[t][:, D:D + 1], 1e-10, 1e-3, ALU.add, ALU.mult))
                    for t in pair:
                        ins = dve.bn_aggr(MV[:, t, :], ST[:, t, :])
                        if t == GT - 1:
                            ins.then_inc(var_ready, 1)
                        else:
                            a[t] = step(ins)
                    for t in pair:
                        if t == GT - 1:
                            dve.wait_ge(var_ready, it * INST + (l * PAIR + g + 1))
                        else:
                            own(it, a[t])
                        dve.scalar_tensor_tensor(O[g][:, t, :], ps[t][:, 0:D], MV[:, t, 0:1], gain[:, l, :],
                                                 ALU.subtract, ALU.mult).then_inc(drained, 1)

            def finish(now, it, l, g):
                dve.wait_ge(sd_ready, it * INST + (l * PAIR + g + 1))
                own(now, step(dve.scalar_tensor_tensor(FC[:, :], SD[:, :], float(np.sqrt(D / (D - 1.0))), WS[:, :], ALU.mult, ALU.add)))
                own(now, step(dve.reciprocal(FC[:, :], FC[:, :])))
                dve.wait_ge(drained, jobs.drained(("C", l, g, GT - 1), it))
                s = {}
                for t in range(GT):
                    ins = dve.scalar_tensor_tensor(O[g][:, t, :], O[g][:, t, :], FC[:, t:t + 1], beta[:, l, :], ALU.mult, ALU.add)
                    if l == LAYERS - 1:
                        s[t] = step(ins)
                if l < LAYERS - 1:
                    ins.then_inc(o_ready, 1)
                    return
                for t in range(GT):
                    own(now, s[t])
                    ins = dve.scalar_tensor_tensor(O[g][:, t, :], O[g][:, t, :], 0.0, X[g][:, t, :], ALU.max, ALU.add)
                    if t == GT - 1:
                        ins.then_inc(x_free[g], 1)
                    else:
                        s[t] = step(ins)
                return s

            def final_statistics(now, it, g, s):
                for t in range(GT):
                    if t == GT - 1:
                        dve.wait_ge(x_free[g], it + 1)
                    else:
                        own(now, s[t])
                    s[t] = step(dve.bn_stats(ST2[:, t, :], O[g][:, t, :]))
                own(now, s[GT - 1])
                dve.tensor_scalar(scratch[:, 2 + g:3 + g], FC[:, 0:1], 0.0, None, ALU.mult)
                for t in range(GT):
                    s[t] = step(dve.bn_aggr(MV2[:, t, :], ST2[:, t, :]))
                own(now, s[GT - 1])
                dve.tensor_scalar(VE[:, :], MV2[:, :, 1], 1e-5, None, ALU.add).then_inc(var2_ready, 1)

            def minus_mean(it, g):
                dve.wait_ge(rs_ready, it * PAIR + (g + 1))
                dve.scalar_tensor_tensor(NB[g][:, :], MV2[:, :, 0], -1.0, RS[g][:, :], ALU.mult, ALU.mult).then_inc(nb_ready, 1)

            def body(it, first=False, last=False):
                count[0] = V_FINISH + V_RESIDUAL if first else 0
                for k in range(INST):
                    l, g = divmod(k, PAIR)
                    nl, ng = following(k)
                    ended = {}
                    split_n(it, l, g, 0)
                    if k == 0 and not first:
                        ended = finish(it, it - 1, LAYERS - 1, 1)
                    for i in range(1, KC):
                        split_n(it, l, g, i)
                    if k:
                        statistics(it, *divmod(k - 1, PAIR))
                    for i in range(KC, 2 * KC):
                        split_n(it, l, g, i)
                    if k:
                        ended = finish(it, it, *divmod(k - 1, PAIR))
                    if k < INST - 1:
                        add_bias(it, l, g, 0)
                    if ended and k == 0:
                        final_statistics(it, it - 1, 1, ended)
                    mask_scores(it, l, g)
                    if k == INST - 1:
                        add_bias(it, l, g, 0)
                    add_bias(it, l, g, 1)
                    add_bias(it, l, g, 2)
                    if k == INST - 1:
                        add_bias(it, l, g, 3)
                    more = not (k == INST - 1 and last)
                    if more and nl == 0:
                        masks(it + (k == INST - 1), ng)
                    if ended and k:
                        final_statistics(it, it, 0, ended)
                    if more:
                        split_t(it + (k == INST - 1), nl, ng)
                    else:
                        for i in EARLY:
                            next_weight(i)
                    if ended:
                        minus_mean(it if k else it - 1, 1 - g)
                    if k < INST - 1:
                        add_bias(it, l, g, 3)
                statistics(it, LAYERS - 1, 1)
                assert count[0] == V_STEPS, (count[0], V_STEPS)

            masks(0, 0)
            split_t(0, 0, 0)
            for m in range(HEAD_MATS, len(mats)):
                split_weight(m)
            dve.wait_ge(c_in, 16 * 3 * LAYERS)
            body(0, first=True)
            with dve.Fori(1, STEPS - 1, 1) as it:
                body(it)
            body(STEPS - 1, last=True)
            count[0] = 0
            next_weight(LATE[0])
            ended = finish(STEPS, STEPS - 1, LAYERS - 1, 1)
            next_weight(LATE[1])
            final_statistics(STEPS, STEPS - 1, 1, ended)
            next_weight(LATE[2])
            minus_mean(STEPS - 1, 1)
            next_weight(LATE[3])

def network1(nc, core, x, adj, b_upper, b_self, b_lower, ln_w, ln_b, out):
    UPPER, LOWER, SELF = range(3)
    def plan(last):
        order = []
        for k in range(INST):
            l, g = divmod(k, PAIR)
            nl, ng = following(k)
            head = [("A", nl, ng, 0)] if nl == 0 else []
            head += [("T", nl, ng, c) for c in range(KC)]
            rows = [[("R", l, g, (t, m)) for m in (UPPER, LOWER, SELF)] for t in range(GT)]
            order += rows[0] + rows[1] + rows[2] + rows[3][:1]
            order += [] if last and k == INST - 1 else head
            order += rows[3][1:]
            order += [("C", l, g, t) for t in range(GT)]
        return order

    HEAD = [("A", 0, 0, 0)] + [("T", 0, 0, c) for c in range(KC)]
    jobs = Plan(plan(False), plan(True), HEAD)
    BT = 2
    SLOTS = 4

    ctx = ExitStack()
    with ctx:
        def sb(name, shape, dt=F32):
            return ctx.enter_context(nc.sbuf_tensor("n1_" + name, shape, dt))

        def sem(name):
            return ctx.enter_context(nc.semaphore("n1_" + name))

        ident, W, X, O, A, bank, ubank = core.ident, core.W, core.X, core.O, core.A, core.bank, core.ubank
        identr, ones = sb("identr", [P, P], F32R), sb("ones", [P, P], F32R)
        cross = sb("cross", [P, BT, 2, P], F32R)
        bias = sb("bias", [P, LAYERS, 3, D])
        gain, beta = (sb(n, [P, LAYERS, D]) for n in ("gain", "beta"))
        AT = sb("at", [P, GT, P])
        AM = [sb(f"am{g}", [P, 3, GT, P]) for g in range(PAIR)]
        HT = [sb(f"ht{g}", [P, 2, KC, GT * P], F32R) for g in range(PAIR)]
        HB = sb("hb", [P, SLOTS, D])
        HL = [sb(f"hl{s}", [P, 2, GT, HLW], F32R) for s in range(2)]
        HS = sb("hs", [P, GT, D])
        MX, NM, NT = sb("mx", [P, GT]), sb("nm", [P, GT], F32R), sb("nt", [P, GT])
        SH = sb("sh", [P, GT, P], F32R)
        HLO = sb("hlo", [P, GT, P], F32R)
        E = sb("e", [P, GT, P])
        EM = sb("em", [P, 2, GT, P])
        ES, DG = sb("es", [P, GT, P]), sb("dg", [P, GT])
        PR = [sb(f"p{s}", [P, 2, GT, P], F32R) for s in range(2)]
        Z = [sb(f"z{g}", [P, GT]) for g in range(PAIR)]
        mhalf = sb("mhalf", [P, GT])
        ST, MV = sb("st", [P, GT, 6]), sb("mv", [P, GT, 2])
        SS, DEN, D2, VV, FC = (sb(n, [P, GT]) for n in ("ss", "den", "d2", "vv", "fc"))
        ST2, MV2, VE = sb("st2", [P, GT, 6]), sb("mv2", [P, GT, 2]), sb("ve", [P, GT])
        RS, NB = ([sb(f"{n}{g}", [P, GT]) for g in range(PAIR)] for n in ("rs", "nb"))
        scratch, scratch2 = sb("scratch", [P, 12]), sb("scratch2", [P, 4, GT])


        bank_full = sem("bank_full")
        drained = sem("drained")
        x_in, a_in = [core.next_x_in, sem("x_in1")], [core.next_a_in, sem("a_in1")]
        x_free, a_free, stored = ([sem(f"{n}{g}") for g in range(PAIR)] for n in ("x_free", "a_free", "stored"))
        ht_hi, u_parts, hlo_done, u_full, u_shifted, z_done = (
            sem(n) for n in ("ht_hi", "u_parts", "hlo_done", "u_full", "u_shifted", "z_done"))
        shift_ready, e_done, em_done, es_done, dg_done, p_hi, p_lo = (
            sem(n) for n in ("shift_ready", "e_done", "em_done", "es_done", "dg_done", "p_hi", "p_lo"))
        hl_hi, hl_lo = sem("hl_hi"), sem("hl_lo")
        var_ready, sd_ready, o_ready, var2_ready, rs_ready, nb_ready, o_out = (
            sem(n) for n in ("var_ready", "sd_ready", "o_ready", "var2_ready", "rs_ready", "nb_ready", "o_out"))
        mx_done, nm_done, bias_ready, den_done = (sem(n) for n in ("mx_done", "nm_done", "bias_ready", "den_done"))
        v_done = sem("v_done")
        c_in, made = sem("c_in"), sem("made")
        identr_made, cross_made = sem("identr_made"), sem("cross_made")

        def score(b, part=0):
            return ubank[b][:, :].rearrange("p (t s i) -> p s t i", t=BT, s=2)[:, part]

        xg = x.rearrange("(g t p) d -> g p t d", p=P, t=GT)
        og = out.rearrange("(g t p) d -> g p t d", p=P, t=GT)
        ag = adj.rearrange("(g t q) j i -> g q j t i", q=2, t=GT)

        block = ctx.enter_context(nc.Block())

        @block.sync
        def _(sp):
            def load(step, g, first=False):
                if not first:
                    sp.wait_ge(a_free[g], step)
                for q in range(2):
                    sp.dma_start(A[g][q * NODES:(q + 1) * NODES, :, q * NODES:(q + 1) * NODES],
                                 ag[step * PAIR + g][q]).then_inc(a_in[g], 16)
                if not first:
                    sp.wait_ge(x_free[g], step)
                sp.dma_start(X[g][:, :, :], xg[step * PAIR + g]).then_inc(x_in[g], 16)

            def store(step, g):
                sp.wait_ge(o_out, step * PAIR + g + 1)
                sp.dma_start(og[step * PAIR + g], O[g][:, :, :]).then_inc(stored[g], 16)

            for l in range(LAYERS):
                for dst, src in ((bias[:, l, UPPER], b_upper), (bias[:, l, LOWER], b_lower), (bias[:, l, SELF], b_self),
                                 (gain[:, l], ln_w), (beta[:, l], ln_b)):
                    sp.dma_start(dst, src[l].partition_broadcast(P)).then_inc(c_in, 16)
            load(0, 1, first=True)
            for g in range(PAIR):
                sp.wait_ge(core.stored[g], core.all_stored)
            with sp.Fori(0, STEPS - 1, 1) as it:
                for g in range(PAIR):
                    load(it + 1, g)
                    store(it, g)
            for g in range(PAIR):
                store(STEPS - 1, g)
            for g in range(PAIR):
                sp.wait_ge(stored[g], (STEPS + 1) * 16)

        @block.tensor
        def _(pe):
            pe.wait_ge(bank_full, jobs.ahead)

            def start(name, it):
                pe.wait_ge(drained, jobs.free(name, it))
                return bank[jobs.bank_of[name]]

            def head(it, l, g):
                if l == 0:
                    pe.wait_ge(a_in[g], (it + 1) * 32)
                    ps = start(("A", l, g, 0), it - (g == 0))
                    for t in range(GT):
                        last = pe.transpose(ps[:, t * P:(t + 1) * P], A[g][:, t, :], ident[:, :])
                    last.then_inc(bank_full, 1)
                    pe.wait_ge(x_in[g], (it + 1) * 16)
                else:
                    pe.wait_ge(o_ready, it * PAIR + g + 1)
                src = X[g] if l == 0 else O[g]
                for c in range(KC):
                    ps = start(("T", l, g, c), it - (l == 0 and g == 0))
                    for t in range(GT):
                        last = pe.transpose(ps[:, t * P:(t + 1) * P], src[:, t, c * P:(c + 1) * P], ident[:, :])
                    before_loop = isinstance(it, int) and it == 0 and l == 0 and g == 0 and c == KC - 1
                    last.then_inc(bank_full, 1 + jobs.behind if before_loop else 1)

            def score_parts(it, l, g):
                for c in range(KC):
                    pe.wait_ge(drained, jobs.drained(("T", l, g, c), it - (l == 0 and g == 0)))
                    for b in range(GT // BT):
                        if c == 0:
                            pe.matmul(ubank[b][:, :], lhsT=identr[:, :], rhs=cross[:, :, :, :].rearrange("p t s i -> p (t s i)"),
                                      start=True, stop=True)
                        for t in range(b * BT, (b + 1) * BT):
                            cols = slice(t * P, (t + 1) * P)
                            last = pe.matmul(ubank[b][:, t % BT * 2 * P:(t % BT + 1) * 2 * P], lhsT=HT[g][:, 0, c, cols],
                                             rhs=HT[g][:, :, c, cols], start=False, stop=(c == KC - 1), skip_group_check=True)
                last.then_inc(u_parts, 1)

            def scores(it, l, g):
                pe.wait_ge(hlo_done, it * INST + (l * PAIR + g + 1))
                for b in range(GT // BT):
                    pe.matmul(score(b), lhsT=identr[:, :], rhs=HLO[:, b * BT:(b + 1) * BT, :],
                              start=False, stop=True, skip_group_check=True)
                    for t in range(b * BT, (b + 1) * BT):
                        last = pe.matmul(score(b)[:, t % BT, :], lhsT=HLO[:, t, :], rhs=identr[:, :],
                                         start=False, stop=True, skip_group_check=True)
                last.then_inc(u_full, 1)

            def shift(it, l, g):
                n = it * INST + (l * PAIR + g)
                pe.wait_ge(shift_ready, n + 1)
                pe.wait_ge(z_done, n + 1)
                for b in range(GT // BT):
                    last = pe.matmul(score(b), lhsT=ones[:, :], rhs=SH[:, b * BT:(b + 1) * BT, :],
                                     start=False, stop=True, skip_group_check=True)
                last.then_inc(u_shifted, 1)

            def project(it, l, g, t, which=(UPPER, LOWER, SELF)):
                for m in which:
                    ps = start(("R", l, g, (t, m)), it)
                    for c in range(KC):
                        for j, (a, b) in enumerate(TERMS):
                            last = pe.matmul(ps[:, 0:D], lhsT=HT[g][:, a, c, t * P:(t + 1) * P],
                                             rhs=W[l][m][b][:, c, :], start=(c == 0 and j == 0), stop=(c == KC - 1 and j == 2))
                    last.then_inc(bank_full, 1)

            def combine(it, l, g, tiles):
                n = it * INST + (l * PAIR + g)
                pe.wait_ge(p_lo, n + 2)
                for t in tiles:
                    ps = start(("C", l, g, t), it)
                    pe.wait_ge(hl_lo, n * (2 * GT) + (2 * t + 2 + SLOTS))
                    for side in (UPPER, LOWER):
                        for j, (a, b) in enumerate(TERMS):
                            last = pe.matmul(ps[:, 0:HLW], lhsT=PR[a][:, side, t, :], rhs=HL[b][:, side, t, :],
                                             start=(side == UPPER and j == 0), stop=(side == LOWER and j == 2))
                    last.then_inc(bank_full, 1)

            def body(it, last=False):
                for k in range(INST):
                    l, g = divmod(k, PAIR)
                    ahead = (it + (k == INST - 1), *following(k))
                    on = not (last and k == INST - 1)
                    project(it, l, g, 0, (UPPER,))
                    shift(it, l, g)
                    project(it, l, g, 0, (LOWER, SELF))
                    project(it, l, g, 1)
                    project(it, l, g, 2)
                    project(it, l, g, 3, (UPPER,))
                    if on:
                        head(*ahead)
                    project(it, l, g, 3, (LOWER, SELF))
                    if on:
                        score_parts(*ahead)
                    combine(it, l, g, range(0, 1))
                    if on:
                        scores(*ahead)
                    combine(it, l, g, range(1, GT))

            head(0, 0, 0)
            pe.wait_ge(identr_made, 1)
            pe.wait_ge(cross_made, 2)
            score_parts(0, 0, 0)
            scores(0, 0, 0)
            pe.wait_ge(made, 1)
            with pe.Fori(0, STEPS - 1, 1) as it:
                body(it)
            body(STEPS - 1, last=True)

        @block.scalar
        def _(act):
            act.activation(identr[:, :], ident[:, :], ACT.Copy).then_inc(identr_made, 1)

            def split_t(it, l, g):
                for c in range(KC):
                    name, step = ("T", l, g, c), it - (l == 0 and g == 0)
                    act.wait_ge(bank_full, jobs.done(name, step))
                    act.activation(HT[g][:, 0, c, :], bank[jobs.bank_of[name]][:, :], ACT.Relu if l else ACT.Copy).then_inc(ht_hi, 1)

            def copy_hlo(it, l, g):
                act.wait_ge(u_parts, it * INST + (l * PAIR + g + 1))
                for b in range(GT // BT):
                    ins = act.activation(HLO[:, b * BT:(b + 1) * BT, :], score(b, 1), ACT.Copy)
                ins.then_inc(hlo_done, 1)

            def row_sums(it, l, g):
                n = it * INST + (l * PAIR + g)
                act.wait_ge(es_done, n + 1)
                act.wait_ge(bias_ready, n + 1)
                for t in range(GT):
                    ins = act.activation(E[:, t, :], score(t // BT)[:, t % BT, :], ACT.Exp, scale=TEMPER, bias=NT[:, t:t + 1],
                                         accum_out=Z[g][:, t:t + 1])
                ins.then_inc(z_done, 1)

            def exps(it, l, g):
                n = it * INST + (l * PAIR + g)
                act.wait_ge(u_shifted, n + 1)
                for b in range(GT // BT):
                    ins = act.activation(E[:, b * BT:(b + 1) * BT, :], score(b), ACT.Exp, scale=TEMPER)
                ins.then_inc(e_done, 1)

            def split_r(it, l, g, t, which=(UPPER, LOWER)):
                for m in which:
                    act.wait_ge(drained, jobs.drained(("R", l, g, (t, m)), it))
                    act.activation(HL[0][:, m, t, 0:D], HB[:, (2 * t + m) % SLOTS, :], ACT.Copy).then_inc(hl_hi, 1)

            def split_p(it, l, g):
                pl, pg = divmod((l * PAIR + g - 1) % INST, PAIR)
                act.wait_ge(em_done, it * INST + (l * PAIR + g + 2))
                act.wait_ge(bank_full, jobs.done(("C", pl, pg, GT - 1), it - (l == 0 and g == 0)))
                act.activation(PR[0][:, :, :, :], EM[:, :, :, :], ACT.Copy).then_inc(p_hi, 1)

            def normalise(it, g):
                act.wait_ge(nb_ready, it * PAIR + (g + 1))
                for t in range(GT):
                    ins = act.activation(O[g][:, t, :], O[g][:, t, :], ACT.Identity, bias=NB[g][:, t:t + 1], scale=RS[g][:, t:t + 1])
                ins.then_inc(o_out, 1)

            def body(it, first=False, last=False):
                for k in range(INST):
                    l, g = divmod(k, PAIR)
                    ahead = (it + (k == INST - 1), *following(k))
                    on = not (last and k == INST - 1)
                    split_r(it, l, g, 0)
                    split_r(it, l, g, 1)
                    split_p(it, l, g)
                    split_r(it, l, g, 2)
                    split_r(it, l, g, 3, (UPPER,))
                    if on:
                        split_t(*ahead)
                    split_r(it, l, g, 3, (LOWER,))
                    if on:
                        copy_hlo(*ahead)
                        row_sums(*ahead)
                        exps(*ahead)
                    if k == 0 and not first:
                        normalise(it - 1, 1)
                    if k == INST - 1:
                        normalise(it, 0)

            split_t(0, 0, 0)
            copy_hlo(0, 0, 0)
            row_sums(0, 0, 0)
            exps(0, 0, 0)
            body(0, first=True)
            with act.Fori(1, STEPS - 1, 1) as it:
                body(it)
            body(STEPS - 1, last=True)
            normalise(STEPS - 1, 1)

        @block.gpsimd
        def _(pool):
            pool.memset(as_f32(ones[:, :]), 1.0)
            pool.memset(scratch2[:, 0, :], 0.0).then_inc(p_lo, 1)
            pool.memset(scratch2[:, 1, :], 0.0).then_inc(es_done, 1)
            pool.memset(mhalf[:, :], -0.5).then_inc(made, 1)
            pool.wait_ge(made, 1)
            pool.memset(as_f32(HL[1][:, :, :, D:HLW]), 0.0)
            pool.memset(as_f32(HL[0][:, :, :, D:HLW]), 1.0).then_inc(hl_lo, SLOTS)

            def carry_wait(k):
                pool.tensor_tensor(scratch2[:, k, :], mhalf[:, :], mhalf[:, :], ALU.mult)

            def masks(it, g):
                if not (isinstance(it, int) and it == 0 and g == 0):
                    pool.wait_ge(em_done, it * INST + (PAIR + g + 2 - INST))
                pool.wait_ge(drained, jobs.drained(("A", 0, g, 0), it - (g == 0)))
                carry_wait(g)
                for m, (op, sign) in enumerate(((ALU.is_gt, 1), (ALU.is_gt, -1), (ALU.is_equal, 1))):
                    ins = pool.affine_select(out=AM[g][:, m], in_=AT[:, :, :], compare_op=op, fill=0.0, base=0,
                                             pattern=[[0, GT], [-sign, P]], channel_multiplier=sign)
                ins.then_inc(a_free[g], 1)

            def split_r(it, l, g, t):
                n = it * INST + (l * PAIR + g)
                for m in (UPPER, LOWER):
                    pool.wait_ge(hl_hi, n * (2 * GT) + (2 * t + m + 1))
                    pool.tensor_tensor(HL[1][:, m, t, 0:D], HB[:, (2 * t + m) % SLOTS, :], as_f32(HL[0][:, m, t, 0:D]),
                                       ALU.subtract).then_inc(hl_lo, 1)

            def diagonal(it, l, g):
                n = it * INST + (l * PAIR + g)
                if l == 0:
                    pool.wait_ge(a_free[g], it + 1)
                pool.wait_ge(dg_done, n + 1)
                pool.wait_ge(e_done, n + 1)
                pool.tensor_tensor(ES[:, :, :], E[:, :, :], AM[g][:, 2], ALU.mult).then_inc(es_done, 1)

            def split_p(it, l, g):
                pool.wait_ge(p_hi, it * INST + (l * PAIR + g + 1))
                pool.tensor_tensor(PR[1][:, :, :, :].rearrange("p s t i -> p (s t i)"), EM[:, :, :, :].rearrange("p s t i -> p (s t i)"),
                                   as_f32(PR[0][:, :, :, :]).rearrange("p s t i -> p (s t i)"), ALU.subtract).then_inc(p_lo, 1)

            def deviation(it, l, g):
                pool.wait_ge(var_ready, it * INST + (l * PAIR + g + 1))
                pool.tensor_tensor(FC[:, :], VV[:, :], mhalf[:, :], ALU.pow).then_inc(sd_ready, 1)

            def final_deviation(it, g):
                pool.wait_ge(var2_ready, it * PAIR + (g + 1))
                pool.tensor_tensor(RS[g][:, :], VE[:, :], mhalf[:, :], ALU.pow).then_inc(rs_ready, 1)

            def body(it, first=False, last=False):
                for k in range(INST):
                    l, g = divmod(k, PAIR)
                    on = not (last and k == INST - 1)
                    diagonal(it, l, g)
                    split_r(it, l, g, 0)
                    split_r(it, l, g, 1)
                    split_p(it, l, g)
                    split_r(it, l, g, 2)
                    split_r(it, l, g, 3)
                    if k == 0 and not first:
                        final_deviation(it - 1, 1)
                    if k == INST - 1:
                        final_deviation(it, 0)
                    if on and following(k)[0] == 0:
                        masks(it + (k == INST - 1), following(k)[1])
                    deviation(it, l, g)

            masks(0, 0)
            body(0, first=True)
            with pool.Fori(1, STEPS - 1, 1) as it:
                body(it)
            body(STEPS - 1, last=True)
            final_deviation(STEPS - 1, 1)

        V_RESIDUAL = 4 * GT - 1
        V_STEPS = INST * (3 * GT + 2) + PAIR * V_RESIDUAL

        @block.vector
        def _(dve):
            dve.memset(scratch[:, 0:1], 0.0).then_inc(drained, CREDIT + jobs.ahead)
            for g in range(PAIR):
                dve.memset(scratch[:, 2 + g:3 + g], 0.0).then_inc(stored[g], 16)
            dve.memset(scratch[:, 4:5], 0.0).then_inc(dg_done, 1)
            dve.memset(scratch[:, 5:6], 0.0).then_inc(em_done, 1)

            dve.memset(scratch[:, 8:9], 0.0).then_inc(v_done, V_RESIDUAL)
            dve.memset(scratch[:, 9:10], 0.0).then_inc(bank_full, jobs.ahead)
            dve.memset(as_f32(cross[:, :, :, :]), 0.0).then_inc(cross_made, 1)
            dve.wait_ge(cross_made, 1)
            dve.memset(as_f32(cross[0:NODES, :, 0, NODES:P]), CROSS)
            dve.memset(as_f32(cross[NODES:P, :, 0, 0:NODES]), CROSS).then_inc(cross_made, 1)
            count = [0]

            def step(ins):
                count[0] += 1
                ins.then_inc(v_done, 1)
                return count[0]

            def own(it, k):
                dve.wait_ge(v_done, it * V_STEPS + k)

            def full(name, it):
                dve.wait_ge(bank_full, jobs.done(name, it))
                return bank[jobs.bank_of[name]]

            def masks(it, g):
                if not (isinstance(it, int) and it == 0 and g == 0):
                    dve.wait_ge(a_free[1 - g], it + g)
                dve.tensor_copy(flat(AT[:, :, :]), full(("A", 0, g, 0), it - (g == 0))[:, :]).then_inc(drained, 1)

            def split_t(it, l, g):
                for c in range(KC):
                    ps = full(("T", l, g, c), it - (l == 0 and g == 0))
                    dve.wait_ge(ht_hi, (it * INST + (l * PAIR + g)) * KC + (c + 1))
                    hi, lo = as_f32(HT[g][:, 0, c, :]), HT[g][:, 1, c, :]
                    before_loop = isinstance(it, int) and it == 0 and l == 0 and g == 0 and c == KC - 1
                    if l == 0:
                        dve.tensor_tensor(lo, ps[:, :], hi, ALU.subtract).then_inc(drained, 1 + jobs.behind if before_loop else 1)
                    else:
                        dve.scalar_tensor_tensor(lo, ps[:, :], 0.0, hi, ALU.max, ALU.subtract).then_inc(drained, 1)

            def maxima(it, l, g):
                n = it * INST + (l * PAIR + g)
                dve.wait_ge(u_full, n + 1)
                for b in range(GT // BT):
                    ins = dve.tensor_reduce(MX[:, b * BT:(b + 1) * BT], score(b), AX.X, ALU.max)
                ins.then_inc(mx_done, 1)
                dve.wait_ge(mx_done, n + 1)
                dve.tensor_scalar(NM[:, :], MX[:, :], -1.0, None, ALU.mult).then_inc(nm_done, 1)
                dve.wait_ge(nm_done, n + 1)
                dve.tensor_scalar(NT[:, :], as_f32(NM[:, :]), TEMPER, None, ALU.mult).then_inc(bias_ready, 1)
                for t in range(GT):
                    ins = dve.tensor_scalar(SH[:, t, :], ident[:, :], as_f32(NM[:, t:t + 1]), None, ALU.mult)
                ins.then_inc(shift_ready, 1)

            def add_bias(it, l, g, t, which=(UPPER, LOWER, SELF)):
                n = it * INST + (l * PAIR + g)
                for m in which:
                    ps = full(("R", l, g, (t, m)), it)
                    if m == SELF:
                        dst = HS[:, t, :]
                    else:
                        dve.wait_ge(hl_lo, n * (2 * GT) + (2 * t + m + 1))
                        dst = HB[:, (2 * t + m) % SLOTS, :]
                    dve.tensor_tensor(dst, ps[:, 0:D], bias[:, l, m], ALU.add).then_inc(drained, 1)

            def mask_exp(it, l, g):
                n = it * INST + (l * PAIR + g)
                if l == 0:
                    dve.wait_ge(a_free[g], it + 1)
                dve.wait_ge(p_lo, n + 1)
                dve.wait_ge(e_done, n + 1)
                for side in (UPPER, LOWER):
                    ins = dve.tensor_tensor(EM[:, side], E[:, :, :], AM[g][:, side], ALU.mult)
                ins.then_inc(em_done, 1)

            def diagonal(it, l, g):
                dve.wait_ge(es_done, it * INST + (l * PAIR + g + 2))
                dve.tensor_reduce(DG[:, :], ES[:, :, :], AX.X, ALU.add).then_inc(dg_done, 1)

            def statistics(it, l, g):
                n = it * INST + (l * PAIR + g)
                dve.wait_ge(dg_done, n + 2)
                dve.wait_ge(drained, jobs.drained(("R", l, g, (GT - 1, SELF)), it))
                if l == 0:
                    dve.wait_ge(stored[g], it * 16 + 16)
                for t in range(GT):
                    ps = full(("C", l, g, t), it)
                    step(dve.tensor_scalar(SS[:, t:t + 1], ps[:, D:D + 1], DG[:, t:t + 1], None, ALU.add))
                    dve.scalar_tensor_tensor(O[g][:, t, :], HS[:, t, :], DG[:, t:t + 1], ps[:, 0:D],
                                             ALU.mult, ALU.add).then_inc(drained, 1)
                for t in range(GT):
                    dve.wait_ge(drained, jobs.drained(("C", l, g, t), it))
                    s = step(dve.bn_stats(ST[:, t, :], O[g][:, t, :]))
                own(it, s)
                dve.tensor_scalar(scratch[:, 6:7], DG[:, 0:1], 0.0, None, ALU.mult)
                for t in range(GT):
                    s = step(dve.bn_aggr(MV[:, t, :], ST[:, t, :]))
                dve.wait_ge(z_done, n + 1)
                dve.scalar_tensor_tensor(DEN[:, :], Z[g][:, :], 1e-10, SS[:, :], ALU.mult, ALU.add).then_inc(den_done, 1)
                dve.wait_ge(den_done, n + 1)
                own(it, step(dve.tensor_tensor(D2[:, :], DEN[:, :], DEN[:, :], ALU.mult)))
                dve.scalar_tensor_tensor(VV[:, :], D2[:, :], 1e-12, MV[:, :, 1], ALU.mult, ALU.add).then_inc(var_ready, 1)
                for t in range(GT):
                    ins = dve.scalar_tensor_tensor(O[g][:, t, :], O[g][:, t, :], MV[:, t, 0:1], gain[:, l, :],
                                                   ALU.subtract, ALU.mult)
                step(ins)

            def finish(now, it, l, g):
                own(now, count[0])
                dve.wait_ge(sd_ready, it * INST + (l * PAIR + g + 1))
                s = {}
                for t in range(GT):
                    ins = dve.scalar_tensor_tensor(O[g][:, t, :], O[g][:, t, :], FC[:, t:t + 1], beta[:, l, :], ALU.mult, ALU.add)
                    if l == LAYERS - 1:
                        s[t] = step(ins)
                if l < LAYERS - 1:
                    ins.then_inc(o_ready, 1)
                    return
                for t in range(GT):
                    own(now, s[t])
                    ins = dve.scalar_tensor_tensor(O[g][:, t, :], O[g][:, t, :], 0.0, X[g][:, t, :], ALU.max, ALU.add)
                    if t == GT - 1:
                        ins.then_inc(x_free[g], 1)
                    else:
                        s[t] = step(ins)
                return s

            def final_statistics(now, it, g, s):
                for t in range(GT):
                    if t == GT - 1:
                        dve.wait_ge(x_free[g], it + 1)
                    else:
                        own(now, s[t])
                    s[t] = step(dve.bn_stats(ST2[:, t, :], O[g][:, t, :]))
                own(now, s[GT - 1])
                dve.tensor_scalar(scratch[:, 10 + g:11 + g], FC[:, 0:1], 0.0, None, ALU.mult)
                for t in range(GT):
                    s[t] = step(dve.bn_aggr(MV2[:, t, :], ST2[:, t, :]))
                own(now, s[GT - 1])
                dve.tensor_scalar(VE[:, :], MV2[:, :, 1], 1e-5, None, ALU.add).then_inc(var2_ready, 1)

            def minus_mean(it, g):
                dve.wait_ge(rs_ready, it * PAIR + (g + 1))
                dve.scalar_tensor_tensor(NB[g][:, :], MV2[:, :, 0], -1.0, RS[g][:, :], ALU.mult, ALU.mult).then_inc(nb_ready, 1)

            def body(it, first=False, last=False):
                count[0] = V_RESIDUAL if first else 0
                for k in range(INST):
                    l, g = divmod(k, PAIR)
                    ahead = (it + (k == INST - 1), *following(k))
                    on = not (last and k == INST - 1)
                    add_bias(it, l, g, 0, (UPPER, LOWER))
                    before, ended = it if k else it - 1, None
                    if k or not first:
                        ended = finish(it, before, *divmod((k - 1) % INST, PAIR))
                    add_bias(it, l, g, 0, (SELF,))
                    add_bias(it, l, g, 1)
                    mask_exp(it, l, g)
                    add_bias(it, l, g, 2)
                    diagonal(it, l, g)
                    add_bias(it, l, g, 3, (UPPER,))
                    if on:
                        if ahead[1] == 0:
                            masks(ahead[0], ahead[2])
                        split_t(*ahead)
                    add_bias(it, l, g, 3, (LOWER, SELF))
                    if ended:
                        final_statistics(it, before, 1 - g, ended)
                    if on:
                        maxima(*ahead)
                    if ended:
                        minus_mean(before, 1 - g)
                    statistics(it, l, g)
                assert count[0] == V_STEPS, (count[0], V_STEPS)

            masks(0, 0)
            split_t(0, 0, 0)
            dve.wait_ge(made, 1)
            maxima(0, 0, 0)
            dve.wait_ge(c_in, 16 * 5 * LAYERS)
            for g in range(PAIR):
                dve.wait_ge(core.stored[g], core.all_stored)
            body(0, first=True)
            with dve.Fori(1, STEPS - 1, 1) as it:
                body(it)
            body(STEPS - 1, last=True)
            count[0] = 0
            ended = finish(STEPS, STEPS - 1, LAYERS - 1, 1)
            final_statistics(STEPS, STEPS - 1, 1, ended)
            minus_mean(STEPS - 1, 1)


NAMES = ["x", "adj", "L0_gnn_W_left", "L0_gnn_W_right", "L0_gnn_W_lin", "L0_gnn_b_lin", "L0_gnn_ln_a", "L0_gnn_ln_b",
         "L1_gnn_Wl", "L1_gnn_bl", "L1_gnn_Ws", "L1_gnn_bs", "L1_gnn_Wr", "L1_gnn_br", "L1_gnn_ln_w", "L1_gnn_ln_b"]


def program(nc, a, x1, out):
    with ExitStack() as ctx:
        core = Core(nc, ctx, (a["L1_gnn_Wl"], a["L1_gnn_Wr"], a["L1_gnn_Ws"]))
        network0(nc, core, a["x"], a["adj"], a["L0_gnn_W_left"], a["L0_gnn_W_right"], a["L0_gnn_W_lin"],
                 a["L0_gnn_b_lin"], a["L0_gnn_ln_a"], a["L0_gnn_ln_b"], x1)
        network1(nc, core, x1, a["adj"], a["L1_gnn_bl"], a["L1_gnn_bs"], a["L1_gnn_br"],
                 a["L1_gnn_ln_w"], a["L1_gnn_ln_b"], out)


def kernel(**inputs):
    import concourse.bacc as bacc
    from concourse.bass_utils import run_bass_kernel_spmd as run
    nc = bacc.Bacc("TRN2", target_bir_lowering=False, num_devices=1)
    arrays, aps = {}, {}
    for name in NAMES:
        v = np.ascontiguousarray(inputs[name])
        if name == "x":
            v = v.reshape(GRAPHS * NODES, D)
        arrays["in_" + name] = v
        aps[name] = nc.dram_tensor("in_" + name, v.shape, F32, kind="ExternalInput").ap()
    x1 = nc.dram_tensor("x1", (GRAPHS * NODES, D), F32, kind="Internal").ap()
    out = nc.dram_tensor("out", (GRAPHS * NODES, D), F32, kind="ExternalOutput").ap()
    program(nc, aps, x1, out)
    r = run(nc, [arrays], core_ids=[0])
    return r.results[0]["out"].reshape(GRAPHS, NODES, D)
```
